# Optimizing a Trainium2 kernel written in Bass

```python
import numpy as np
import jax
import jax.numpy as jnp

def _softmax(x, axis=-1):
    return jax.nn.softmax(x, axis=axis)

def _gelu(x):
    return jax.nn.gelu(x, approximate=True)

def _silu(x):
    return jax.nn.silu(x)

def _sigmoid(x):
    return jax.nn.sigmoid(x)

def _layernorm(x, axis=-1, eps=1e-05):
    m = jnp.mean(x, axis=axis, keepdims=True)
    v = jnp.var(x, axis=axis, keepdims=True)
    return (x - m) / jnp.sqrt(v + eps)

def _scatter_add(tgt, idx, src, axis=0):
    return tgt.at[idx].add(src)

def _segment_sum(src, seg, n):
    return jax.ops.segment_sum(src, seg, n)
kernel_name = 'mk_adj_ffn_d1_adj_r2_95f1c1'

def setup_inputs(seed: int=0):
    np.random.seed(seed)
    _w = jnp.asarray

    def _rec_inputs():
        import jax
        import jax.numpy as jnp
        _gk = jax.random.key(seed)
        x = 7.22e-05 + 1 * jax.random.normal(jax.random.fold_in(_gk, 1), (32, 256, 128), jnp.float32)
        _a = jax.random.bernoulli(jax.random.fold_in(_gk, 2), 0.015625, (32, 256, 256))
        _a = jnp.logical_or(_a, jnp.swapaxes(_a, -1, -2))
        _a = jnp.logical_or(_a, jnp.eye(256, dtype=bool))
        _af = _a.astype(jnp.float32)
        _af = _af * jax.random.uniform(jax.random.fold_in(_gk, 3), (32, 256, 256), jnp.float32, 0.05, 1)
        adj = _af
        return (x, adj)
    x, adj = _rec_inputs()

    def _L0_gnn_setup():
        import jax, jax.numpy as jnp
        import numpy as np
        D_IN = 128
        D_HID = 256
        key = jax.random.key(seed)
        k1, k2, k3, k4, k5, k6 = jax.random.split(key, 6)
        x = jax.random.normal(k1, (8, 2048, D_IN), dtype=jnp.float32)
        adj = jax.random.uniform(k2, (8, 2048, 2048), dtype=jnp.float32)
        s1 = 1.0 / np.sqrt(D_IN)
        s2 = 1.0 / np.sqrt(D_HID)
        W1 = jax.random.uniform(k3, (D_IN, D_HID), dtype=jnp.float32, minval=-s1, maxval=s1)
        b1 = jax.random.uniform(k4, (D_HID,), dtype=jnp.float32, minval=-s1, maxval=s1)
        W2 = jax.random.uniform(k5, (D_HID, D_IN), dtype=jnp.float32, minval=-s2, maxval=s2)
        b2 = jax.random.uniform(k6, (D_IN,), dtype=jnp.float32, minval=-s2, maxval=s2)
        eps = jnp.zeros((1,), dtype=jnp.float32)
        return {'x': x, 'adj': adj, 'eps': eps, 'W1': W1, 'b1': b1, 'W2': W2, 'b2': b2}
    _L0_gnn_all = _L0_gnn_setup()
    _L0_gnn_in = {k: v for k, v in _L0_gnn_all.items() if k in ('eps', 'W1', 'b1', 'W2', 'b2')}
    del _L0_gnn_all

    def _L0_ffn_setup():
        import jax, jax.numpy as jnp
        import numpy as np
        NUM_EXPERTS = 8
        TOP_K = 2
        B, S, D = (8, 4096, 128)

        def _moe(tokens, router_w, w1, b1, w2, b2):
            N = tokens.shape[0]
            E = router_w.shape[0]
            logits = tokens.astype(jnp.float32) @ router_w.astype(jnp.float32).T
            probs = jax.nn.softmax(logits, axis=-1)
            rw, re = jax.lax.top_k(probs, TOP_K)
            if TOP_K > 1:
                rw = rw / jnp.maximum(rw.sum(-1, keepdims=True), 1e-12)
            rw = rw.astype(tokens.dtype)
            combine = jnp.zeros((N, E), tokens.dtype).at[jnp.arange(N)[:, None], re].set(rw)
            out = tokens
            for e in range(E):
                h = jax.nn.gelu(tokens @ w1[e] + b1[e], approximate=False)
                y = h @ w2[e] + b2[e]
                out = out + combine[:, e:e + 1] * y
            return out
        key = jax.random.key(seed)
        ks = jax.random.split(key, 4)
        scale = 1.0 / np.sqrt(D).astype(np.float32)
        return {'input_embeddings': jax.random.normal(ks[0], (B, S, D), jnp.float32), 'router_w': jax.random.normal(ks[1], (NUM_EXPERTS, D), jnp.float32) * scale, 'w1': jax.random.normal(ks[2], (NUM_EXPERTS, D, D), jnp.float32) * scale, 'b1': jnp.zeros((NUM_EXPERTS, D), jnp.float32), 'w2': jax.random.normal(ks[3], (NUM_EXPERTS, D, D), jnp.float32) * scale, 'b2': jnp.zeros((NUM_EXPERTS, D), jnp.float32)}
    _L0_ffn_all = _L0_ffn_setup()
    _L0_ffn_in = {k: v for k, v in _L0_ffn_all.items() if k in ('router_w', 'w1', 'b1', 'w2', 'b2')}
    del _L0_ffn_all
    return {'x': x, 'adj': adj, 'L0_gnn_eps': _L0_gnn_in['eps'], 'L0_gnn_W1': _L0_gnn_in['W1'], 'L0_gnn_b1': _L0_gnn_in['b1'], 'L0_gnn_W2': _L0_gnn_in['W2'], 'L0_gnn_b2': _L0_gnn_in['b2'], 'L0_ffn_router_w': _L0_ffn_in['router_w'], 'L0_ffn_w1': _L0_ffn_in['w1'], 'L0_ffn_b1': _L0_ffn_in['b1'], 'L0_ffn_w2': _L0_ffn_in['w2'], 'L0_ffn_b2': _L0_ffn_in['b2']}

def reference(x, adj, L0_gnn_eps, L0_gnn_W1, L0_gnn_b1, L0_gnn_W2, L0_gnn_b2, L0_ffn_router_w, L0_ffn_w1, L0_ffn_b1, L0_ffn_w2, L0_ffn_b2):
    import jax
    import jax.numpy as jnp

    def _L0_gnn_ref(x, adj, eps, W1, b1, W2, b2):
        import jax, jax.numpy as jnp
        import numpy as np
        D_IN = 128
        D_HID = 256
        aggregated = jnp.einsum('bnm,bmd->bnd', adj, x)
        h = (1.0 + eps) * x + aggregated
        h = jax.nn.relu(h @ W1 + b1)
        return h @ W2 + b2

    def _L0_ffn_ref(input_embeddings, router_w, w1, b1, w2, b2):
        import jax, jax.numpy as jnp
        import numpy as np
        NUM_EXPERTS = 8
        TOP_K = 2
        B, S, D = (8, 4096, 128)

        def _moe(tokens, router_w, w1, b1, w2, b2):
            N = tokens.shape[0]
            E = router_w.shape[0]
            logits = tokens.astype(jnp.float32) @ router_w.astype(jnp.float32).T
            probs = jax.nn.softmax(logits, axis=-1)
            rw, re = jax.lax.top_k(probs, TOP_K)
            if TOP_K > 1:
                rw = rw / jnp.maximum(rw.sum(-1, keepdims=True), 1e-12)
            rw = rw.astype(tokens.dtype)
            combine = jnp.zeros((N, E), tokens.dtype).at[jnp.arange(N)[:, None], re].set(rw)
            out = tokens
            for e in range(E):
                h = jax.nn.gelu(tokens @ w1[e] + b1[e], approximate=False)
                y = h @ w2[e] + b2[e]
                out = out + combine[:, e:e + 1] * y
            return out
        b, s, d = input_embeddings.shape
        tokens = input_embeddings.reshape(b * s, d)
        return _moe(tokens, router_w, w1, b1, w2, b2).reshape(b, s, d)
    x = x + _L0_gnn_ref(_layernorm(x, axis=-1), adj, L0_gnn_eps, L0_gnn_W1, L0_gnn_b1, L0_gnn_W2, L0_gnn_b2)
    x = x + _L0_ffn_ref(_layernorm(x, axis=-1), L0_ffn_router_w, L0_ffn_w1, L0_ffn_b1, L0_ffn_w2, L0_ffn_b2)
    return x

_drawn_inputs = setup_inputs


def setup_inputs(seed=0):
    import zlib

    import numpy as np

    out = dict(_drawn_inputs(seed))
    spreads = {'L0_ffn_b1': (0.0, 0.344), 'L0_ffn_b2': (0.0, 0.1)}
    factors = {}
    for name, (base, spread) in spreads.items():
        noise = np.random.default_rng([zlib.crc32(name.encode()), seed]).standard_normal(out[name].shape)
        drawn = base * np.exp(spread * noise) if base else spread * noise
        out[name] = jnp.asarray(drawn.astype(out[name].dtype))
    for name, factor in factors.items():
        out[name] = (out[name] * factor).astype(out[name].dtype)
    return out
```

```python
from contextlib import ExitStack

import concourse.bass as bass
from concourse import mybir

ALU = mybir.AluOpType
ACT = mybir.ActivationFunctionType
F32 = mybir.dt.float32
F32R = mybir.dt.float32r
AX_X = mybir.AxisListType.X

P = 128
LN_EPS = 1e-5
PROB_FLOOR = 1e-12
EULER = 2.718281828459045


class Step:

    def __init__(self, k, c):
        self.k, self.c = k, c

    def at(self, off):
        return Step(self.k, self.c + off)

    @property
    def parity(self):
        return self.c % 2

    def index(self):
        return self.count(1, 0)

    def count(self, per_group, plus):
        fixed = per_group * self.c + plus
        return fixed if self.k is None else self.k * (2 * per_group) + fixed

    def loads(self):
        fixed = 16 * (self.c // 2 + 1)
        return fixed if self.k is None else self.k * 16 + fixed


def gnn_moe_block(nc, x, adj, eps, W1, b1, W2, b2, router_w, w1, mb1, w2, mb2, out):
    G, N, D = x.shape
    H = W1.shape[1]
    E = router_w.shape[0]
    HC = H // P
    NC = N // P
    T = 4
    GG = T // NC
    GROUPS = G // GG
    TOK = T * P
    assert D == P and N == NC * P and H == HC * P and GG * NC == T and GROUPS % 2 == 0
    C2 = 2 * E

    x_rows = x.rearrange("g (c p) d -> p (g c) d", p=P)
    out_rows = out.rearrange("g (c p) d -> p (g c) d", p=P)
    adj_rows = adj.rearrange("g (c p) m -> p (g c) m", p=P)

    ctx = ExitStack()
    with ctx:
        def sb(name, shape, dt=F32):
            return ctx.enter_context(nc.sbuf_tensor(name, shape, dt))

        def psum(name, shape):
            return ctx.enter_context(nc.psum_tensor(name, shape, F32))

        def sem(name):
            return ctx.enter_context(nc.semaphore(name))

        ident = sb("ident", [P, P])
        diag = sb("diag", [P, NC, N])
        eps1 = sb("eps1", [P, 1])
        half = sb("half", [P, T])
        minus = sb("minus", [P, T])
        ln_eps = sb("ln_eps", [P, T])
        euler = sb("euler", [P, T, E])
        W1_sb = sb("W1_sb", [P, H])
        b1_rows = sb("b1_rows", [HC, P])
        b1_sb = sb("b1_sb", [P, HC])
        W2_sb = sb("W2_sb", [P, HC, D])
        b2_bc = sb("b2_bc", [P, D])
        rw_sb = sb("rw_sb", [E, D])
        rwT = sb("rwT", [P, E])
        rwT_hi = sb("rwT_hi", [P, E], F32R)
        rwT_lo = sb("rwT_lo", [P, E], F32R)
        w1_sb = sb("w1_sb", [P, E, D])
        w1_hi = sb("w1_hi", [P, E, D], F32R)
        w1_lo = sb("w1_lo", [P, E, D], F32R)
        w2_sb = sb("w2_sb", [P, E, D])
        mb1_sb = sb("mb1_sb", [E, D])
        mb1T = sb("mb1T", [P, E])
        mb2_sb = sb("mb2_sb", [C2, D])
        mb2_hi = sb("mb2_hi", [C2, D], F32R)
        mb2_lo = sb("mb2_lo", [C2, D], F32R)
        sel_f = sb("sel_f", [C2, E, P])
        sel = sb("sel", [C2, E, P], F32R)

        x_sb = sb("x_sb", [P, 2, T, D])
        adj_sb = sb("adj_sb", [P, 2, T, N])
        mv1 = sb("mv1", [P, T, 2])
        st1 = sb("st1", [P, T, 6])
        nm1 = sb("nm1", [P, T])
        ve1 = sb("ve1", [P, T])
        rs1 = sb("rs1", [P, T])
        xn = sb("xn", [P, T, D])
        xb = sb("xb", [P, T, D])
        adjT = sb("adjT", [P, GG, NC, N])
        aT = sb("aT", [P, TOK])
        hT = sb("hT", [P, HC, TOK])
        x1 = sb("x1", [P, T, D])
        st2 = sb("st2", [P, T, 6])
        mv2 = sb("mv2", [P, T, 2])
        ve2 = sb("ve2", [P, T])
        rs2 = sb("rs2", [P, T])
        z = sb("z", [P, T, D])
        res = sb("res", [P, 2, T, D])
        zT_hi = sb("zT_hi", [P, 2, TOK], F32R)
        zT_lo = sb("zT_lo", [P, 2, TOK], F32R)
        lmax = sb("lmax", [P, T])
        lsub = sb("lsub", [P, T, E])
        pexp = sb("pexp", [P, T, E])
        psum_e = sb("psum_e", [P, T])
        prec = sb("prec", [P, T])
        prob = sb("prob", [P, T, C2])
        top = sb("top", [P, T, 8])
        rest = sb("rest", [P, T, C2])
        chosen = sb("chosen", [P, T, E])
        tsum = sb("tsum", [P, T])
        tsafe = sb("tsafe", [P, T])
        trec = sb("trec", [P, T])
        cw = sb("cw", [P, T, E])
        c_parts = sb("c_parts", [P, T, C2])
        cT = sb("cT", [C2, TOK], F32R)
        g_sb = sb("g_sb", [P, 3, TOK])
        gc = sb("gc", [P, 3, TOK])
        accT = sb("accT", [P, TOK])
        o_sb = sb("o_sb", [P, T, D])

        wait_cell = sb("wait_cell", [P, 2])

        bankA = psum("bankA", [P, TOK])
        bankB = psum("bankB", [P, TOK])
        bankO = psum("bankO", [P, TOK])
        bankH = [psum(f"bankH{j}", [P, TOK]) for j in range(2)]
        bankC = [psum(f"bankC{j}", [P, TOK]) for j in range(2)]
        bankY = psum("bankY", [P, TOK])

        wl = sem("weights_landed")
        pool_const = sem("pool_const")
        setup_t = sem("setup_transposes")
        setup_dve = sem("setup_dve")
        x_in = [sem(f"x_in{j}") for j in range(2)]
        adj_in = [sem(f"adj_in{j}") for j in range(2)]
        ln1_sub = sem("ln1_sub")
        ln1_stats = sem("ln1_stats")
        ln1_small = sem("ln1_small")
        xn_ready = sem("xn_ready")
        xb_ready = sem("xb_ready")
        adjT_ps = sem("adjT_ps")
        adjT_ready = sem("adjT_ready")
        agg_ps = sem("agg_ps")
        aT_ready = sem("aT_ready")
        f1_ps = sem("f1_ps")
        hT_ready = sem("hT_ready")
        f2_ps = sem("f2_ps")
        x1_ready = sem("x1_ready")
        ln2_sub = sem("ln2_sub")
        ln2_stats = sem("ln2_stats")
        ln2_small = sem("ln2_small")
        rs2_ready = sem("rs2_ready")
        z_ready = sem("z_ready")
        res_ready = sem("res_ready")
        zT_ps = sem("zT_ps")
        zhi_ready = sem("zhi_ready")
        zlo_ready = sem("zlo_ready")
        lg_ps = sem("lg_ps")
        lsub_ready = sem("lsub_ready")
        lmax_ready = sem("lmax_ready")
        pexp_ready = sem("pexp_ready")
        top_step = sem("top_step")
        c_ready = sem("c_ready")
        cT_ps = sem("cT_ps")
        cT_ready = sem("cT_ready")
        cb_ps = sem("cb_ps")
        h_ps = sem("h_ps")
        g_ready = sem("g_ready")
        gc_ready = sem("gc_ready")
        w2_done = sem("w2_done")
        accT_ready = sem("accT_ready")
        o_ps = sem("o_ps")
        o_ready = sem("o_ready")
        o_stored = sem("o_stored")

        WEIGHT_LOADS = 12
        TOP_STEPS = 10

        block = ctx.enter_context(nc.Block())

        def run(eng, iteration):
            iteration(Step(None, 0))
            with eng.Fori(0, (GROUPS - 4) // 2) as k:
                for p in range(2):
                    iteration(Step(k, 1 + p))
            for i in range(GROUPS - 3, GROUPS):
                iteration(Step(None, i))

        def fixed(s):
            return s.c if s.k is None else None

        def has(s, off):
            return s.k is not None or 0 <= s.c + off < GROUPS

        @block.sync
        def _(sp):
            def rows(n, array):
                view = array[:, bass.ds(n.index() * T, T), :]
                if n.k is not None:
                    sp.lower_val(view.offset * 4)
                return view

            def ahead(*values):
                for v in values:
                    if not isinstance(v, int):
                        sp.lower_val(v)

            def load(n, x_view, adj_view):
                sp.dma_start(x_sb[:, n.parity], x_view).then_inc(x_in[n.parity], 16)
                sp.dma_start(adj_sb[:, n.parity], adj_view).then_inc(adj_in[n.parity], 16)

            load(Step(None, 0), rows(Step(None, 0), x_rows), rows(Step(None, 0), adj_rows))
            sp.dma_start(eps1[:], eps.partition_broadcast(P)).then_inc(wl, 16)
            sp.dma_start(W1_sb[:], W1).then_inc(wl, 16)
            sp.dma_start(b1_rows[:], b1.rearrange("(j p) -> j p", p=P)).then_inc(wl, 16)
            sp.dma_start(W2_sb[:], W2.rearrange("(j p) d -> p j d", p=P)).then_inc(wl, 16)
            sp.dma_start(b2_bc[:], b2.partition_broadcast(P)).then_inc(wl, 16)
            sp.dma_start(rw_sb[:], router_w).then_inc(wl, 16)
            sp.dma_start(mb1_sb[:], mb1).then_inc(wl, 16)
            sp.dma_start(mb2_sb[0:E, :], mb2).then_inc(wl, 16)
            sp.dma_start(mb2_sb[E:C2, :], mb2).then_inc(wl, 16)
            sp.dma_start(w1_sb[:, 0:E // 2], w1[0:E // 2].rearrange("e d f -> d e f")).then_inc(wl, 16)
            sp.dma_start(w1_sb[:, E // 2:E], w1[E // 2:E].rearrange("e d f -> d e f")).then_inc(wl, 16)
            sp.dma_start(w2_sb[:], w2.rearrange("e f d -> f e d")).then_inc(wl, 16)
            load(Step(None, 1), rows(Step(None, 1), x_rows), rows(Step(None, 1), adj_rows))

            def store(m, out_view):
                sp.wait_ge(o_ready, m.count(1, 1))
                sp.dma_start(out_view, o_sb[:]).then_inc(o_stored, 16)

            def iteration(i):
                if has(i, 2):
                    x_view, adj_view = rows(i.at(2), x_rows), rows(i.at(2), adj_rows)
                if has(i, -1):
                    out_view = rows(i.at(-1), out_rows)
                ahead(i.count(1, 1), i.count(GG, GG), i.count(1, 0))
                if has(i, 2):
                    sp.wait_ge(xb_ready, i.count(1, 1))
                    sp.wait_ge(xn_ready, i.count(1, 1))
                    sp.wait_ge(adjT_ps, i.count(GG, GG))
                    load(i.at(2), x_view, adj_view)
                if has(i, -1):
                    store(i.at(-1), out_view)

            run(sp, iteration)
            store(Step(None, GROUPS - 1), rows(Step(None, GROUPS - 1), out_rows))
            sp.wait_ge(o_stored, 16 * GROUPS)

        @block.gpsimd
        def _(pool):
            def const(ins):
                const.n += 1
                ins.then_inc(pool_const, 1)
                pool.wait_ge(pool_const, const.n)

            const.n = 0
            const(nc.gpsimd.memset(ident[:], 0.0))
            const(nc.gpsimd.affine_select(out=ident[:], in_=ident[:], compare_op=ALU.not_equal, fill=1.0, base=0,
                                          pattern=[[-1, P]], channel_multiplier=1))
            const(nc.gpsimd.memset(half[:], -0.5))
            const(nc.gpsimd.memset(minus[:], -1.0))
            const(nc.gpsimd.memset(ln_eps[:], LN_EPS))
            const(nc.gpsimd.memset(euler[:], EULER))
            const(nc.gpsimd.memset(sel_f[:], 0.0))
            for base in (0, -E):
                const(nc.gpsimd.affine_select(out=sel_f[:], in_=sel_f[:], compare_op=ALU.not_equal, fill=1.0,
                                              base=base, pattern=[[-1, E], [0, P]], channel_multiplier=1))
            const(nc.gpsimd.memset(prob[:], -1.0))
            const(nc.gpsimd.memset(diag[:], 0.0))
            pool.wait_ge(wl, 16 * WEIGHT_LOADS)
            const(nc.gpsimd.tensor_scalar(eps1[:], eps1[:], 1.0, None, ALU.add))
            for c in range(NC):
                const(nc.gpsimd.tensor_scalar(diag[:, c, c * P:(c + 1) * P], ident[:], eps1[:, 0:1], None, ALU.mult))
            assert const.n == 14

            def ln1(n):
                pool.wait_ge(ln1_stats, n.count(1, 1))
                pool.wait_ge(agg_ps, n.count(1, 0))
                nc.gpsimd.tensor_tensor(ve1[:], mv1[:, :, 1], ln_eps[:], ALU.add).then_inc(ln1_small, 1)
                nc.gpsimd.tensor_tensor(nm1[:], mv1[:, :, 0], minus[:], ALU.mult).then_inc(ln1_small, 1)
                pool.wait_ge(ln1_small, n.count(3, 2))
                nc.gpsimd.tensor_tensor(rs1[:], ve1[:], half[:], ALU.pow).then_inc(ln1_small, 1)
                pool.wait_ge(x1_ready, n.count(1, 0))
                pool.wait_ge(ln1_small, n.count(3, 3))
                nc.gpsimd.tensor_tensor(xb[:], x_sb[:, n.parity],
                                        b2_bc[:].unsqueeze(1).to_broadcast([P, T, D]), ALU.add).then_inc(xb_ready, 1)
                for t in range(T):
                    last = nc.gpsimd.tensor_scalar(xn[:, t, :], x_sb[:, n.parity, t, :], nm1[:, t:t + 1],
                                                   rs1[:, t:t + 1], ALU.add, ALU.mult)
                last.then_inc(xn_ready, 1)

            def ln2(n):
                pool.wait_ge(ln2_stats, n.count(1, 1))
                nc.gpsimd.tensor_tensor(ve2[:], mv2[:, :, 1], ln_eps[:], ALU.add).then_inc(ln2_small, 1)
                pool.wait_ge(ln2_small, n.count(1, 1))
                nc.gpsimd.tensor_tensor(rs2[:], ve2[:], half[:], ALU.pow).then_inc(rs2_ready, 1)

            def residual(n, reader):
                pool.wait_ge(z_ready, n.count(1, 1))
                if reader:
                    pool.wait_ge(o_ready, n.count(1, -1))
                nc.gpsimd.tensor_tensor(res[:, n.parity], x1[:], z[:], ALU.add).then_inc(res_ready, 1)

            def exps(n):
                pool.wait_ge(lsub_ready, n.count(1, 1))
                nc.gpsimd.tensor_tensor(pexp[:], euler[:], lsub[:], ALU.pow).then_inc(pexp_ready, 1)

            first = Step(None, 0)
            ln1(first)
            ln2(first)
            residual(first, False)
            exps(first)
            ln1(first.at(1))

            def iteration(i):
                n = i.at(1)
                if has(i, 1):
                    ln2(n)
                    residual(n, has(i, -1))
                    exps(n)
                if has(i, 2):
                    ln1(i.at(2))

            run(pool, iteration)

        @block.scalar
        def _(act):
            def aggT_copy(n):
                act.wait_ge(agg_ps, n.count(1, 1))
                act.wait_ge(f1_ps, n.count(HC, 0))
                nc.scalar.activation(aT[:], bankA[:], ACT.Copy).then_inc(aT_ready, 1)

            def hidden_relu(n, j):
                act.wait_ge(f1_ps, n.count(HC, j + 1))
                act.wait_ge(f2_ps, n.count(1, 0))
                bank = (bankB, bankA)[j]
                nc.scalar.activation(hT[:, j, :], bank[:], ACT.Relu, bias=b1_sb[:, j:j + 1]).then_inc(hT_ready, 1)

            def z_high(n, again):
                act.wait_ge(zT_ps, n.count(1, 1))
                if again:
                    act.wait_ge(h_ps, n.count(E, -E))
                nc.scalar.activation(zT_hi[:, n.parity], bankA[:], ACT.Copy).then_inc(zhi_ready, 1)

            def cT_copy(n):
                act.wait_ge(cT_ps, n.count(1, 1))
                act.wait_ge(cb_ps, n.count(E, 0))
                act.wait_ge(w2_done, n.count(E, 0))
                nc.scalar.activation(cT[:], bankA[0:C2, :], ACT.Copy).then_inc(cT_ready, 1)

            def gelu(i, e):
                act.wait_ge(h_ps, i.count(E, e + 1))
                if e >= 3:
                    act.wait_ge(gc_ready, i.count(E, e - 2))
                else:
                    act.wait_ge(gc_ready, i.count(E, 0))
                nc.scalar.activation(g_sb[:, e % 3, :], bankH[e % 2][:], ACT.Gelu,
                                     bias=mb1T[:, e:e + 1]).then_inc(g_ready, 1)

            def accT_copy(i):
                act.wait_ge(w2_done, i.count(E, E))
                act.wait_ge(o_ps, i.count(1, 0))
                nc.scalar.activation(accT[:], bankY[:], ACT.Copy).then_inc(accT_ready, 1)

            act.wait_ge(wl, 16 * WEIGHT_LOADS)
            act.wait_ge(setup_dve, 11)
            first = Step(None, 0)
            aggT_copy(first)
            for j in range(HC):
                hidden_relu(first, j)
            z_high(first, False)
            cT_copy(first)

            def iteration(i):
                n = i.at(1)
                more = has(i, 1)
                gelu(i, 0)
                gelu(i, 1)
                if more:
                    aggT_copy(n)
                gelu(i, 2)
                if more:
                    for j in range(HC):
                        hidden_relu(n, j)
                gelu(i, 3)
                gelu(i, 4)
                gelu(i, 5)
                if more:
                    z_high(n, has(i, -1))
                gelu(i, 6)
                gelu(i, 7)
                accT_copy(i)
                if more:
                    cT_copy(n)

            run(act, iteration)

        @block.vector
        def _(dve):
            def ln1_stat(n):
                dve.wait_ge(x_in[n.parity], n.loads())
                for t in range(T):
                    last = nc.vector.bn_stats(st1[:, t, :], x_sb[:, n.parity, t, :])
                last.then_inc(ln1_sub, 1)
                dve.wait_ge(ln1_sub, n.count(1, 1))
                dve.wait_ge(xn_ready, n.count(1, 0))
                nc.vector.memset(wait_cell[:], 0.0)
                for t in range(T):
                    last = nc.vector.bn_aggr(mv1[:, t, :], st1[:, t, :])
                last.then_inc(ln1_stats, 1)

            def adjT_evac(n, g):
                dve.wait_ge(adjT_ps, n.count(GG, g + 1))
                dve.wait_ge(agg_ps, n.count(1, 0))
                bank = (bankA, bankB)[g]
                nc.vector.tensor_tensor(adjT[:, g], bank[:].rearrange("p (c n) -> p c n", c=NC), diag[:],
                                        ALU.add).then_inc(adjT_ready, 1)

            def first_residual(n):
                dve.wait_ge(f2_ps, n.count(1, 1))
                dve.wait_ge(xb_ready, n.count(1, 1))
                dve.wait_ge(res_ready, n.count(1, 0))
                nc.vector.tensor_tensor(x1[:], bankB[:].rearrange("p (t d) -> p t d", t=T), xb[:],
                                        ALU.add).then_inc(x1_ready, 1)
                dve.wait_ge(x1_ready, n.count(1, 1))
                for t in range(T):
                    last = nc.vector.bn_stats(st2[:, t, :], x1[:, t, :])
                last.then_inc(ln2_sub, 1)
                dve.wait_ge(ln2_sub, n.count(1, 1))
                nc.vector.memset(wait_cell[:], 0.0)
                for t in range(T):
                    last = nc.vector.bn_aggr(mv2[:, t, :], st2[:, t, :])
                last.then_inc(ln2_stats, 1)
                dve.wait_ge(ln2_stats, n.count(1, 1))

            def ln2_apply(n):
                dve.wait_ge(rs2_ready, n.count(1, 1))
                dve.wait_ge(zT_ps, n.count(1, 0))
                for t in range(T):
                    last = nc.vector.tensor_scalar(z[:, t, :], x1[:, t, :], mv2[:, t, 0:1], rs2[:, t:t + 1],
                                                   ALU.subtract, ALU.mult)
                last.then_inc(z_ready, 1)

            def z_low(n):
                dve.wait_ge(zhi_ready, n.count(1, 1))
                nc.vector.tensor_tensor(zT_lo[:, n.parity], bankA[:], zT_hi[:, n.parity].bitcast(F32),
                                        ALU.subtract).then_inc(zlo_ready, 1)

            def softmax_top(n):
                dve.wait_ge(lg_ps, n.count(1, 1))
                logits = bankB[:, 0:T * E].rearrange("p (t e) -> p t e", t=T)
                nc.vector.tensor_reduce(lmax[:], logits, AX_X, ALU.max).then_inc(lmax_ready, 1)
                dve.wait_ge(lmax_ready, n.count(1, 1))
                nc.vector.tensor_tensor(lsub[:], logits, lmax[:].unsqueeze(2).to_broadcast([P, T, E]),
                                        ALU.subtract).then_inc(lsub_ready, 1)

            def combine_weights(n):
                done = [0]

                def step(ins):
                    done[0] += 1
                    ins.then_inc(top_step, 1)
                    dve.wait_ge(top_step, n.count(TOP_STEPS, done[0]))

                def wide(a):
                    return a[:].unsqueeze(2).to_broadcast([P, T, E])

                probs = prob[:, :, 0:E]
                dve.wait_ge(pexp_ready, n.count(1, 1))
                step(nc.vector.tensor_reduce(psum_e[:], pexp[:], AX_X, ALU.add))
                step(nc.vector.reciprocal(prec[:], psum_e[:]))
                step(nc.vector.tensor_tensor(probs, pexp[:], wide(prec), ALU.mult))
                nc.vector.memset(wait_cell[:], 0.0)
                for t in range(T):
                    last = nc.vector.max(top[:, t, :], prob[:, t, :])
                step(last)
                nc.vector.tensor_tensor(tsum[:], top[:, :, 0], top[:, :, 1], ALU.add)
                step(nc.vector.memset(top[:, :, 2:8], -1.0))
                nc.vector.tensor_scalar(tsafe[:], tsum[:], PROB_FLOOR, None, ALU.max)
                for t in range(T):
                    last = nc.vector.match_replace(rest[:, t, :], top[:, t, :], prob[:, t, :], 0.0)
                step(last)
                nc.vector.reciprocal(trec[:], tsafe[:])
                step(nc.vector.tensor_tensor(chosen[:], probs, rest[:, :, 0:E], ALU.subtract))
                step(nc.vector.tensor_tensor(cw[:], chosen[:], wide(trec), ALU.mult))
                dve.wait_ge(cT_ps, n.count(1, 0))
                step(nc.vector.tensor_copy(c_parts[:, :, 0:E].bitcast(F32R), cw[:]))
                step(nc.vector.tensor_tensor(c_parts[:, :, E:C2], cw[:], c_parts[:, :, 0:E], ALU.subtract))
                assert done[0] == TOP_STEPS

            def weigh(i, e):
                dve.wait_ge(g_ready, i.count(E, e + 1))
                dve.wait_ge(cb_ps, i.count(E, e + 1))
                if e >= 3:
                    dve.wait_ge(w2_done, i.count(E, e - 2))
                else:
                    dve.wait_ge(w2_done, i.count(E, 0))
                nc.vector.tensor_tensor(gc[:, e % 3, :], g_sb[:, e % 3, :], bankC[e % 2][:],
                                        ALU.mult).then_inc(gc_ready, 1)

            def output(m):
                dve.wait_ge(o_ps, m.count(1, 1))
                dve.wait_ge(res_ready, m.count(1, 1))
                dve.wait_ge(o_stored, m.count(16, 0))
                nc.vector.tensor_tensor(o_sb[:], bankO[:].rearrange("p (t d) -> p t d", t=T), res[:, m.parity],
                                        ALU.add).then_inc(o_ready, 1)

            def setup(ins):
                setup.n += 1
                ins.then_inc(setup_dve, 1)
                dve.wait_ge(setup_dve, setup.n)

            setup.n = 0
            first = Step(None, 0)
            ln1_stat(first)
            dve.wait_ge(setup_t, 1)
            setup(nc.vector.tensor_copy(rwT[:], bankO[:, 0:E]))
            setup(nc.vector.tensor_copy(mb1T[:], bankO[:, E:2 * E]))
            setup(nc.vector.tensor_copy(b1_sb[:], bankO[:, 2 * E:2 * E + HC]))
            setup(nc.vector.tensor_copy(rwT_hi[:], rwT[:]))
            setup(nc.vector.tensor_tensor(rwT_lo[:], rwT[:], rwT_hi[:].bitcast(F32), ALU.subtract))
            setup(nc.vector.tensor_copy(w1_hi[:], w1_sb[:]))
            setup(nc.vector.tensor_tensor(w1_lo[:], w1_sb[:], w1_hi[:].bitcast(F32), ALU.subtract))
            setup(nc.vector.tensor_copy(mb2_hi[:], mb2_sb[:]))
            setup(nc.vector.tensor_tensor(mb2_lo[:], mb2_sb[:], mb2_hi[:].bitcast(F32), ALU.subtract))
            dve.wait_ge(pool_const, 14)
            setup(nc.vector.tensor_copy(sel[:], sel_f[:]))
            setup(nc.vector.memset(c_parts[:], 0.0))

            for g in range(GG):
                adjT_evac(first, g)
            first_residual(first)
            ln2_apply(first)
            z_low(first)
            softmax_top(first)
            combine_weights(first)
            ln1_stat(first.at(1))

            def iteration(i):
                n = i.at(1)
                more = has(i, 1)
                weigh(i, 0)
                if has(i, -1):
                    output(i.at(-1))
                if more:
                    for g in range(GG):
                        adjT_evac(n, g)
                weigh(i, 1)
                weigh(i, 2)
                weigh(i, 3)
                if more:
                    first_residual(n)
                weigh(i, 4)
                if more:
                    ln2_apply(n)
                weigh(i, 5)
                if more:
                    z_low(n)
                weigh(i, 6)
                if more:
                    softmax_top(n)
                weigh(i, 7)
                if more:
                    combine_weights(n)
                if has(i, 2):
                    ln1_stat(i.at(2))

            run(dve, iteration)
            output(Step(None, GROUPS - 1))

        @block.tensor
        def _(pe):
            def mm(out_ap, lhsT, rhs, start, stop):
                return nc.tensor.matmul(out_ap, lhsT, rhs, start=start, stop=stop)

            def three(out_ap, w_hi, w_lo, m_hi, m_lo, start, stop):
                mm(out_ap, w_lo, m_hi, start, False)
                mm(out_ap, w_hi, m_lo, False, False)
                return mm(out_ap, w_hi, m_hi, False, stop)

            def adj_transposes(n):
                pe.wait_ge(adj_in[n.parity], n.loads())
                for g in range(GG):
                    if g == 0:
                        pe.wait_ge(cT_ready, n.count(1, 0))
                    else:
                        pe.wait_ge(lsub_ready, n.count(1, 0))
                    bank = (bankA, bankB)[g]
                    for c in range(NC):
                        for r in range(NC):
                            last = nc.tensor.transpose(bank[:, c * N + r * P:c * N + (r + 1) * P],
                                                       adj_sb[:, n.parity, g * NC + r, c * P:(c + 1) * P], ident[:])
                    last.then_inc(adjT_ps, 1)

            def aggregate(n):
                pe.wait_ge(xn_ready, n.count(1, 1))
                pe.wait_ge(adjT_ready, n.count(GG, GG))
                for g in range(GG):
                    for c in range(NC):
                        last = mm(bankA[:, g * N:(g + 1) * N], xn[:, g * NC + c, :], adjT[:, g, c, :],
                                  c == 0, c == NC - 1)
                last.then_inc(agg_ps, 1)

            def ffn1(n):
                pe.wait_ge(aT_ready, n.count(1, 1))
                for j in range(HC):
                    mm((bankB, bankA)[j][:], W1_sb[:, j * P:(j + 1) * P], aT[:], True, True).then_inc(f1_ps, 1)

            def ffn2(n):
                pe.wait_ge(hT_ready, n.count(HC, HC))
                for t in range(T):
                    for j in range(HC):
                        last = mm(bankB[:, t * D:(t + 1) * D], hT[:, j, t * P:(t + 1) * P], W2_sb[:, j, :],
                                  j == 0, j == HC - 1)
                last.then_inc(f2_ps, 1)

            def z_transposes(n):
                pe.wait_ge(z_ready, n.count(1, 1))
                for t in range(T):
                    last = nc.tensor.transpose(bankA[:, t * P:(t + 1) * P], z[:, t, :], ident[:])
                last.then_inc(zT_ps, 1)

            def router(n):
                pe.wait_ge(zhi_ready, n.count(1, 1))
                pe.wait_ge(zlo_ready, n.count(1, 1))
                for t in range(T):
                    cols = slice(t * P, (t + 1) * P)
                    last = three(bankB[:, t * E:(t + 1) * E], zT_hi[:, n.parity, cols], zT_lo[:, n.parity, cols],
                                 rwT_hi[:], rwT_lo[:], True, True)
                last.then_inc(lg_ps, 1)

            def weight_transposes(n):
                pe.wait_ge(top_step, n.count(TOP_STEPS, TOP_STEPS))
                for t in range(T):
                    last = nc.tensor.transpose(bankA[0:C2, t * P:(t + 1) * P], c_parts[:, t, :], ident[:])
                last.then_inc(cT_ps, 1)

            def spread(i, e):
                if e >= 2:
                    pe.wait_ge(gc_ready, i.count(E, e - 1))
                else:
                    pe.wait_ge(gc_ready, i.count(E, 0))
                    pe.wait_ge(cT_ready, i.count(1, 1))
                mm(bankC[e % 2][:], sel[:, e, :], cT[:], True, True).then_inc(cb_ps, 1)

            def up(i, e):
                if e >= 2:
                    pe.wait_ge(g_ready, i.count(E, e - 1))
                else:
                    pe.wait_ge(g_ready, i.count(E, 0))
                    pe.wait_ge(zhi_ready, i.count(1, 1))
                    pe.wait_ge(zlo_ready, i.count(1, 1))
                three(bankH[e % 2][:], w1_hi[:, e, :], w1_lo[:, e, :], zT_hi[:, i.parity], zT_lo[:, i.parity],
                      True, True).then_inc(h_ps, 1)

            def down(i, e):
                pe.wait_ge(gc_ready, i.count(E, e + 1))
                if e == 0:
                    pe.wait_ge(accT_ready, i.count(1, 0))
                    mm(bankY[:], mb2_lo[:], cT[:], True, False)
                    mm(bankY[:], mb2_hi[:], cT[:], False, False)
                last = mm(bankY[:], w2_sb[:, e, :], gc[:, e % 3, :], False, e == E - 1)
                last.then_inc(w2_done, 1)

            def output_transposes(m):
                pe.wait_ge(accT_ready, m.count(1, 1))
                pe.wait_ge(o_ready, m.count(1, 0))
                for t in range(T):
                    last = nc.tensor.transpose(bankO[:, t * P:(t + 1) * P], accT[:, t * P:(t + 1) * P], ident[:])
                last.then_inc(o_ps, 1)

            pe.wait_ge(pool_const, 2)
            pe.wait_ge(wl, 16 * WEIGHT_LOADS)
            nc.tensor.transpose(bankO[:, 0:E], rw_sb[:], ident[0:E, 0:E])
            nc.tensor.transpose(bankO[:, E:2 * E], mb1_sb[:], ident[0:E, 0:E])
            nc.tensor.transpose(bankO[:, 2 * E:2 * E + HC], b1_rows[:], ident[0:HC, 0:HC]).then_inc(setup_t, 1)
            pe.wait_ge(setup_dve, 11)
            first = Step(None, 0)
            adj_transposes(first)
            aggregate(first)
            ffn1(first)
            ffn2(first)
            z_transposes(first)
            router(first)
            weight_transposes(first)

            def iteration(i):
                n = i.at(1)
                more = has(i, 1)
                up(i, 0)
                if has(i, -1):
                    output_transposes(i.at(-1))
                spread(i, 0)
                if more:
                    adj_transposes(n)
                up(i, 1)
                spread(i, 1)
                if more:
                    aggregate(n)
                up(i, 2)
                spread(i, 2)
                down(i, 0)
                if more:
                    ffn1(n)
                up(i, 3)
                spread(i, 3)
                down(i, 1)
                if more:
                    ffn2(n)
                up(i, 4)
                spread(i, 4)
                down(i, 2)
                up(i, 5)
                spread(i, 5)
                down(i, 3)
                if more:
                    z_transposes(n)
                up(i, 6)
                spread(i, 6)
                down(i, 4)
                if more:
                    router(n)
                up(i, 7)
                spread(i, 7)
                down(i, 5)
                down(i, 6)
                down(i, 7)
                if more:
                    weight_transposes(n)

            run(pe, iteration)
            output_transposes(Step(None, GROUPS - 1))


_INS = ['x', 'adj', 'L0_gnn_eps', 'L0_gnn_W1', 'L0_gnn_b1', 'L0_gnn_W2', 'L0_gnn_b2', 'L0_ffn_router_w',
        'L0_ffn_w1', 'L0_ffn_b1', 'L0_ffn_w2', 'L0_ffn_b2']


def kernel(**inputs):
    import numpy as _np
    import concourse.bacc as _bacc
    from concourse import mybir as _mybir
    from concourse.bass_utils import run_bass_kernel_spmd as _run

    nc = _bacc.Bacc("TRN2", target_bir_lowering=False, num_devices=1)
    arrays, args = {}, []
    for name in _INS:
        a = _np.ascontiguousarray(inputs[name])
        arrays[f"in_{name}"] = a
        args.append(nc.dram_tensor(f"in_{name}", a.shape, _mybir.dt.from_np(a.dtype), kind="ExternalInput").ap())
    shape = inputs['x'].shape
    args.append(nc.dram_tensor("out_0", shape, _mybir.dt.from_np(_np.dtype('float32')), kind="ExternalOutput").ap())
    gnn_moe_block(nc, *args)
    r = _run(nc, [arrays], core_ids=[0])
    return r.results[0]["out_0"]
```

```python
from contextlib import ExitStack

import concourse.bass as bass
from concourse import mybir

ALU = mybir.AluOpType
ACT = mybir.ActivationFunctionType
F32 = mybir.dt.float32
F32R = mybir.dt.float32r
AX_X = mybir.AxisListType.X

P = 128
LN_EPS = 1e-5
LOWEST = -3.0e38


class Step:

    def __init__(self, k, c):
        self.k, self.c = k, c

    def at(self, off):
        return Step(self.k, self.c + off)

    @property
    def parity(self):
        return self.c % 2

    def index(self):
        return self.count(1, 0)

    def count(self, per_group, plus):
        fixed = per_group * self.c + plus
        return fixed if self.k is None else self.k * (2 * per_group) + fixed

    def loads(self):
        fixed = 16 * (self.c // 2 + 1)
        return fixed if self.k is None else self.k * 16 + fixed


def gnn_moe_block(nc, x, adj, eps, W1, b1, W2, b2, router_w, w1, mb1, w2, mb2_rows, out):
    G, N, D = x.shape
    H = W1.shape[1]
    E = router_w.shape[0]
    HC = H // P
    NC = N // P
    T = 4
    GG = T // NC
    GROUPS = G // GG
    TOK = T * P
    assert D == P and N == NC * P and H == HC * P and GG * NC == T and GROUPS % 2 == 0
    ROW_TILE = 32
    CR = 2 * ROW_TILE

    x_rows = x.rearrange("g (c p) d -> p (g c) d", p=P)
    out_rows = out.rearrange("g (c p) d -> p (g c) d", p=P)
    adj_rows = adj.rearrange("g (c p) m -> p (g c) m", p=P)

    ctx = ExitStack()
    with ctx:
        def sb(name, shape, dt=F32):
            return ctx.enter_context(nc.sbuf_tensor(name, shape, dt))

        def psum(name, shape):
            return ctx.enter_context(nc.psum_tensor(name, shape, F32))

        def sem(name):
            return ctx.enter_context(nc.semaphore(name))

        ident = sb("ident", [P, P])
        diag = sb("diag", [P, P])
        eps1 = sb("eps1", [P, 1])
        half = sb("half", [P, T])
        minus = sb("minus", [P, T])
        ln_eps = sb("ln_eps", [P, T])
        W1_sb = sb("W1_sb", [P, H])
        W1_hi = sb("W1_hi", [P, H], F32R)
        W1_lo = sb("W1_lo", [P, H], F32R)
        b1_rows = sb("b1_rows", [HC, P])
        b1_sb = sb("b1_sb", [P, HC])
        W2_sb = sb("W2_sb", [P, HC, D])
        b2_bc = sb("b2_bc", [P, D])
        rw_sb = sb("rw_sb", [E, D])
        rwT = sb("rwT", [P, E])
        rwT_parts = sb("rwT_parts", [P, 2 * E], F32R)
        w1_sb = sb("w1_sb", [P, E, D])
        w1_hi = sb("w1_hi", [P, E, D], F32R)
        w1_lo = sb("w1_lo", [P, E, D], F32R)
        w2_sb = sb("w2_sb", [P, E, D])
        w2_hi = sb("w2_hi", [P, E, D], F32R)
        w2_lo = sb("w2_lo", [P, E, D], F32R)
        mb1_sb = sb("mb1_sb", [E, D])
        mb1T = sb("mb1T", [P, E])
        mb2_sb = sb("mb2_sb", [CR, D])
        mb2 = sb("mb2_parts", [CR, D], F32R)
        sel_f = sb("sel_f", [CR, E, P])
        sel = sb("sel", [CR, E, P], F32R)

        x_sb = sb("x_sb", [P, 2, T, D])
        adj_sb = sb("adj_sb", [P, 2, T, N])
        st1 = sb("st1", [P, T, 6])
        mv1 = sb("mv1", [P, T, 2])
        nm1 = sb("nm1", [P, T])
        ve1 = sb("ve1", [P, T])
        rs1 = sb("rs1", [P, T])
        xn = sb("xn", [P, T, D])
        xb = sb("xb", [P, T, D])
        adjT = sb("adjT", [P, GG, NC, N])
        aT_hi = sb("aT_hi", [P, TOK], F32R)
        aT_lo = sb("aT_lo", [P, TOK], F32R)
        hT = sb("hT", [P, HC, TOK])
        x1 = sb("x1", [P, T, D])
        st2 = sb("st2", [P, T, 6])
        mv2 = sb("mv2", [P, T, 2])
        ve2 = sb("ve2", [P, T])
        rs2 = sb("rs2", [P, T])
        z = sb("z", [P, T, D])
        res = sb("res", [P, 2, T, D])
        zT_hi = sb("zT_hi", [P, 2, TOK], F32R)
        zT_lo = sb("zT_lo", [P, 2, TOK], F32R)
        lg = sb("lg", [P, T, 2 * E])
        top = sb("top", [P, T, 8])
        gap = sb("gap", [P, T])
        th = sb("th", [P, T])
        rest = sb("rest", [P, T, 2 * E])
        chosen = sb("chosen", [P, T, E])
        first_e = sb("first_e", [P, T, E])
        tilt = sb("tilt", [P, T, E])
        cw = sb("cw", [P, T, E])
        c_parts = sb("c_parts", [P, T, P])
        cT = sb("cT", [CR, TOK], F32R)
        g_sb = sb("g_sb", [P, 2, TOK])
        gc = sb("gc", [P, 2, TOK])
        gc_hi = sb("gc_hi", [P, 4, TOK], F32R)
        gc_lo = sb("gc_lo", [P, 4, TOK], F32R)
        yT = sb("yT", [P, TOK])
        o_sb = sb("o_sb", [P, T, D])
        wait_cell = sb("wait_cell", [P, 2])

        bankA = psum("bankA", [P, TOK])
        bankB = psum("bankB", [P, TOK])
        bankO = psum("bankO", [P, TOK])
        bankH = [psum(f"bankH{j}", [P, TOK]) for j in range(2)]
        bankC = [psum(f"bankC{j}", [P, TOK]) for j in range(2)]
        bankY = psum("bankY", [P, TOK])

        gnn_weights = sem("gnn_weights")
        w1_landed = sem("w1_landed")
        w2_landed = sem("w2_landed")
        b2_rows = sem("b2_rows")
        eps_landed = sem("eps_landed")
        w_high = sem("w_high")
        w2_split = sem("w2_split")
        pool_const = sem("pool_const")
        small_T_ps = sem("small_T_ps")
        setup_dve = sem("setup_dve")
        x_in = [sem(f"x_in{j}") for j in range(2)]
        adj_in = [sem(f"adj_in{j}") for j in range(2)]
        ln1_sub = sem("ln1_sub")
        ln1_stats = sem("ln1_stats")
        ln1_small = sem("ln1_small")
        xn_ready = sem("xn_ready")
        xb_ready = sem("xb_ready")
        self_added = sem("self_added")
        adjT_ps = sem("adjT_ps")
        adjT_ready = sem("adjT_ready")
        agg_ps = sem("agg_ps")
        ahi_ready = sem("ahi_ready")
        alo_ready = sem("alo_ready")
        f1_ps = sem("f1_ps")
        hT_ready = sem("hT_ready")
        f2_ps = sem("f2_ps")
        x1_ready = sem("x1_ready")
        ln2_sub = sem("ln2_sub")
        ln2_stats = sem("ln2_stats")
        ln2_small = sem("ln2_small")
        rs2_ready = sem("rs2_ready")
        z_ready = sem("z_ready")
        res_ready = sem("res_ready")
        zT_ps = sem("zT_ps")
        zhi_ready = sem("zhi_ready")
        zlo_ready = sem("zlo_ready")
        lg_ps = sem("lg_ps")
        lg_ready = sem("lg_ready")
        gap_ready = sem("gap_ready")
        th_ready = sem("th_ready")
        top_step = sem("top_step")
        cT_ps = sem("cT_ps")
        cT_ready = sem("cT_ready")
        cb_ps = sem("cb_ps")
        h_ps = sem("h_ps")
        g_ready = sem("g_ready")
        gc_ready = sem("gc_ready")
        hi_ready = sem("hi_ready")
        lo_ready = sem("lo_ready")
        down_done = sem("down_done")
        yT_ready = sem("yT_ready")
        o_ps = sem("o_ps")
        o_ready = sem("o_ready")
        o_stored = sem("o_stored")

        GNN_LOADS, CLEARED, CONSTS, SMALL_SETUPS, SETUPS, TOP_STEPS = 6, 6, 15, 7, 11, 9

        block = ctx.enter_context(nc.Block())

        def run(eng, iteration):
            iteration(Step(None, 0))
            iteration(Step(None, 1))
            with eng.Fori(0, (GROUPS - 4) // 2) as k:
                iteration(Step(k, 2))
                iteration(Step(k, 3))
            iteration(Step(None, GROUPS - 2))
            iteration(Step(None, GROUPS - 1))

        def has(s, off):
            return s.k is not None or 0 <= s.c + off < GROUPS

        def after(eng, what, count):
            if not isinstance(count, int) or count > 0:
                eng.wait_ge(what, count)

        @block.sync
        def _(sp):
            def rows(n, array):
                view = array[:, bass.ds(n.index() * T, T), :]
                if n.k is not None:
                    sp.lower_val(view.offset * 4)
                return view

            def load(n, x_view, adj_view):
                sp.dma_start(x_sb[:, n.parity], x_view).then_inc(x_in[n.parity], 16)
                sp.dma_start(adj_sb[:, n.parity], adj_view).then_inc(adj_in[n.parity], 16)

            def store(m, out_view):
                sp.wait_ge(o_ready, m.count(1, 1))
                sp.dma_start(out_view, o_sb[:]).then_inc(o_stored, 16)

            for n in (Step(None, 0), Step(None, 1)):
                load(n, rows(n, x_rows), rows(n, adj_rows))

            def iteration(i):
                if i.k is not None:
                    sp.lower_val(i.count(1, 1))
                    sp.lower_val(i.count(GG, GG))
                    sp.lower_val(i.count(1, 0))
                if has(i, 2):
                    x_view, adj_view = rows(i.at(2), x_rows), rows(i.at(2), adj_rows)
                if has(i, -1):
                    out_view = rows(i.at(-1), out_rows)
                if has(i, 2):
                    sp.wait_ge(xb_ready, i.count(1, 1))
                    sp.wait_ge(xn_ready, i.count(1, 1))
                    sp.wait_ge(adjT_ps, i.count(GG, GG))
                    load(i.at(2), x_view, adj_view)
                if has(i, -1):
                    store(i.at(-1), out_view)

            run(sp, iteration)
            last = Step(None, GROUPS - 1)
            store(last, rows(last, out_rows))
            sp.wait_ge(o_stored, 16 * GROUPS)

        @block.gpsimd
        def _(pool):
            def const(ins):
                const.n += 1
                ins.then_inc(pool_const, 1)
                pool.wait_ge(pool_const, const.n)

            def ln1(n):
                pool.wait_ge(ln1_stats, n.count(1, 1))
                after(pool, agg_ps, n.count(1, 0))
                nc.gpsimd.tensor_tensor(ve1[:], mv1[:, :, 1], ln_eps[:], ALU.add).then_inc(ln1_small, 1)
                nc.gpsimd.tensor_tensor(nm1[:], mv1[:, :, 0], minus[:], ALU.mult).then_inc(ln1_small, 1)
                pool.wait_ge(ln1_small, n.count(3, 2))
                nc.gpsimd.tensor_tensor(rs1[:], ve1[:], half[:], ALU.pow).then_inc(ln1_small, 1)
                after(pool, x1_ready, n.count(1, 0))
                pool.wait_ge(ln1_small, n.count(3, 3))
                nc.gpsimd.tensor_tensor(xb[:], x_sb[:, n.parity],
                                        b2_bc[:].unsqueeze(1).to_broadcast([P, T, D]), ALU.add).then_inc(xb_ready, 1)
                for t in range(T):
                    last = nc.gpsimd.tensor_scalar(xn[:, t, :], x_sb[:, n.parity, t, :], nm1[:, t:t + 1],
                                                   rs1[:, t:t + 1], ALU.add, ALU.mult)
                last.then_inc(xn_ready, 1)

            def add_self(n):
                pool.wait_ge(adj_in[n.parity], n.loads())
                graphs = adj_sb[:, n.parity].rearrange("p (g c) m -> p g c m", g=GG)
                for c in range(NC):
                    block_c = graphs[:, :, c, c * P:(c + 1) * P]
                    nc.gpsimd.tensor_tensor(block_c, block_c, diag[:].unsqueeze(1).to_broadcast([P, GG, P]),
                                            ALU.add).then_inc(self_added, 1)

            def ln2(n):
                pool.wait_ge(ln2_stats, n.count(1, 1))
                nc.gpsimd.tensor_tensor(ve2[:], mv2[:, :, 1], ln_eps[:], ALU.add).then_inc(ln2_small, 1)
                pool.wait_ge(ln2_small, n.count(1, 1))
                nc.gpsimd.tensor_tensor(rs2[:], ve2[:], half[:], ALU.pow).then_inc(rs2_ready, 1)

            def residual(n):
                pool.wait_ge(z_ready, n.count(1, 1))
                after(pool, o_ready, n.count(1, -1))
                nc.gpsimd.tensor_tensor(res[:, n.parity], x1[:], z[:], ALU.add).then_inc(res_ready, 1)

            const.n = 0
            const(nc.gpsimd.memset(ident[:], 0.0))
            const(nc.gpsimd.affine_select(out=ident[:], in_=ident[:], compare_op=ALU.not_equal, fill=1.0, base=0,
                                          pattern=[[-1, P]], channel_multiplier=1))
            const(nc.gpsimd.memset(half[:], -0.5))
            const(nc.gpsimd.memset(minus[:], -1.0))
            const(nc.gpsimd.memset(ln_eps[:], LN_EPS))
            const(nc.gpsimd.memset(mb2_sb[:], 0.0))
            assert const.n == CLEARED
            pool.wait_ge(eps_landed, 16)
            const(nc.gpsimd.tensor_scalar(eps1[:], eps1[:], 1.0, None, ALU.add))
            const(nc.gpsimd.tensor_scalar(diag[:], ident[:], eps1[:, 0:1], None, ALU.mult))
            first = Step(None, 0)
            add_self(first)
            pool.wait_ge(gnn_weights, 16 * GNN_LOADS)
            ln1(first)
            const(nc.gpsimd.memset(sel_f[:], 0.0))
            for q in range(2):
                for part in range(2):
                    mine = sel_f[:].rearrange("r (h q) p -> r h q p", q=2)[:, :, q, :]
                    const(nc.gpsimd.affine_select(out=mine, in_=mine, compare_op=ALU.not_equal, fill=1.0,
                                                  base=-(ROW_TILE + 1) * q - E * part,
                                                  pattern=[[-2, E // 2], [0, P]], channel_multiplier=1))
            const(nc.gpsimd.memset(lg[:], LOWEST))
            const(nc.gpsimd.memset(c_parts[:], 0.0))
            assert const.n == CONSTS
            add_self(first.at(1))
            ln2(first)
            ln1(first.at(1))
            residual(first)

            def iteration(i):
                if has(i, 2):
                    add_self(i.at(2))
                if has(i, 1):
                    ln2(i.at(1))
                if has(i, 2):
                    ln1(i.at(2))
                if has(i, 1):
                    residual(i.at(1))

            run(pool, iteration)

        @block.scalar
        def _(act):
            def adjT_copy(n, g):
                act.wait_ge(adjT_ps, n.count(GG, g + 1))
                after(act, agg_ps, n.count(1, 0))
                nc.scalar.activation(adjT[:, g].rearrange("p c n -> p (c n)"), (bankA, bankB)[g][:],
                                     ACT.Copy).then_inc(adjT_ready, 1)

            def aT_copy(n):
                act.wait_ge(agg_ps, n.count(1, 1))
                after(act, f1_ps, n.count(HC, 0))
                nc.scalar.activation(aT_hi[:], bankA[:], ACT.Copy).then_inc(ahi_ready, 1)

            def hidden_relu(n, j):
                act.wait_ge(f1_ps, n.count(HC, j + 1))
                after(act, f2_ps, n.count(1, 0))
                nc.scalar.activation(hT[:, j, :], (bankB, bankA)[j][:], ACT.Relu,
                                     bias=b1_sb[:, j:j + 1]).then_inc(hT_ready, 1)

            def z_high(n):
                act.wait_ge(zT_ps, n.count(1, 1))
                after(act, h_ps, n.count(E, -E))
                nc.scalar.activation(zT_hi[:, n.parity], bankA[:], ACT.Copy).then_inc(zhi_ready, 1)

            def gap_tanh(n):
                act.wait_ge(gap_ready, n.count(1, 1))
                nc.scalar.activation(th[:], gap[:], ACT.Tanh, scale=0.5).then_inc(th_ready, 1)

            def cT_copy(n):
                act.wait_ge(cT_ps, n.count(1, 1))
                after(act, cb_ps, n.count(E, 0))
                after(act, down_done, n.count(E, 1 - E))
                nc.scalar.activation(cT[:], bankO[0:CR, :], ACT.Copy).then_inc(cT_ready, 1)

            def gelu(i, e):
                act.wait_ge(h_ps, i.count(E, e + 1))
                after(act, gc_ready, i.count(E, e - 1))
                nc.scalar.activation(g_sb[:, e % 2, :], bankH[e % 2][:], ACT.Gelu,
                                     bias=mb1T[:, e:e + 1]).then_inc(g_ready, 1)

            def high(i, e):
                act.wait_ge(gc_ready, i.count(E, e + 1))
                after(act, down_done, i.count(E, e - 3))
                nc.scalar.activation(gc_hi[:, e % 4, :], gc[:, e % 2, :], ACT.Copy).then_inc(hi_ready, 1)

            def yT_copy(i):
                act.wait_ge(down_done, i.count(E, E))
                after(act, o_ps, i.count(1, 0))
                nc.scalar.activation(yT[:], bankY[:], ACT.Copy).then_inc(yT_ready, 1)

            act.dma_start(eps1[:], eps.partition_broadcast(P)).then_inc(eps_landed, 16)
            act.dma_start(b2_bc[:], b2.partition_broadcast(P)).then_inc(gnn_weights, 16)
            act.dma_start(b1_rows[:], b1.rearrange("(j p) -> j p", p=P)).then_inc(gnn_weights, 16)
            act.dma_start(rw_sb[:], router_w).then_inc(gnn_weights, 16)
            act.dma_start(mb1_sb[:], mb1).then_inc(gnn_weights, 16)
            act.dma_start(W1_sb[:], W1).then_inc(gnn_weights, 16)
            act.dma_start(W2_sb[:], W2.rearrange("(j p) d -> p j d", p=P)).then_inc(gnn_weights, 16)
            act.dma_start(w1_sb[:], w1.rearrange("e d f -> d e f")).then_inc(w1_landed, 16)
            act.dma_start(w2_sb[:], w2.rearrange("e f d -> f e d")).then_inc(w2_landed, 16)
            act.wait_ge(pool_const, CLEARED)
            for row in (0, E, ROW_TILE, ROW_TILE + E):
                act.dma_start(mb2_sb[row:row + E, :], mb2_rows).then_inc(b2_rows, 16)

            first = Step(None, 0)
            for g in range(GG):
                adjT_copy(first, g)
            act.wait_ge(w1_landed, 16)
            nc.scalar.activation(w1_hi[:], w1_sb[:], ACT.Copy).then_inc(w_high, 1)
            aT_copy(first)
            act.wait_ge(setup_dve, SMALL_SETUPS)
            for j in range(HC):
                hidden_relu(first, j)
            act.wait_ge(w2_landed, 16)
            nc.scalar.activation(w2_hi[:], w2_sb[:], ACT.Copy).then_inc(w_high, 1)
            z_high(first)
            gap_tanh(first)
            for g in range(GG):
                adjT_copy(first.at(1), g)

            def iteration(i):
                b, n, f = i.at(-1), i.at(1), i.at(2)
                before, more, further = has(i, -1), has(i, 1), has(i, 2)
                if before:
                    gelu(b, 7)
                    high(b, 6)
                if more:
                    aT_copy(n)
                cT_copy(i)
                gelu(i, 0)
                if before:
                    high(b, 7)
                gelu(i, 1)
                if more:
                    hidden_relu(n, 0)
                    hidden_relu(n, 1)
                high(i, 0)
                high(i, 1)
                gelu(i, 2)
                gelu(i, 3)
                if before:
                    yT_copy(b)
                gelu(i, 4)
                high(i, 2)
                high(i, 3)
                gelu(i, 5)
                if more:
                    z_high(n)
                high(i, 4)
                gelu(i, 6)
                if further:
                    adjT_copy(f, 0)
                    adjT_copy(f, 1)
                if more:
                    gap_tanh(n)
                high(i, 5)

            run(act, iteration)
            last = Step(None, GROUPS - 1)
            gelu(last, 7)
            high(last, 6)
            high(last, 7)
            yT_copy(last)

        @block.vector
        def _(dve):
            def ln1_stat(n):
                dve.wait_ge(x_in[n.parity], n.loads())
                for t in range(T):
                    last = nc.vector.bn_stats(st1[:, t, :], x_sb[:, n.parity, t, :])
                last.then_inc(ln1_sub, 1)
                after(dve, xn_ready, n.count(1, 0))
                dve.wait_ge(ln1_sub, n.count(1, 1))
                nc.vector.memset(wait_cell[:], 0.0)
                for t in range(T):
                    last = nc.vector.bn_aggr(mv1[:, t, :], st1[:, t, :])
                last.then_inc(ln1_stats, 1)

            def a_low(n):
                dve.wait_ge(ahi_ready, n.count(1, 1))
                nc.vector.tensor_tensor(aT_lo[:], bankA[:], aT_hi[:].bitcast(F32), ALU.subtract).then_inc(alo_ready, 1)

            def first_residual(n):
                dve.wait_ge(f2_ps, n.count(1, 1))
                dve.wait_ge(xb_ready, n.count(1, 1))
                after(dve, res_ready, n.count(1, 0))
                nc.vector.tensor_tensor(x1[:], bankB[:].rearrange("p (t d) -> p t d", t=T), xb[:],
                                        ALU.add).then_inc(x1_ready, 1)

            def ln2_stat(n):
                dve.wait_ge(x1_ready, n.count(1, 1))
                for t in range(T):
                    last = nc.vector.bn_stats(st2[:, t, :], x1[:, t, :])
                last.then_inc(ln2_sub, 1)
                dve.wait_ge(ln2_sub, n.count(1, 1))
                nc.vector.memset(wait_cell[:], 0.0)
                for t in range(T):
                    last = nc.vector.bn_aggr(mv2[:, t, :], st2[:, t, :])
                last.then_inc(ln2_stats, 1)

            def ln2_apply(n):
                dve.wait_ge(rs2_ready, n.count(1, 1))
                dve.wait_ge(ln2_stats, n.count(1, 1))
                after(dve, zT_ps, n.count(1, 0))
                for t in range(T):
                    last = nc.vector.tensor_scalar(z[:, t, :], x1[:, t, :], mv2[:, t, 0:1], rs2[:, t:t + 1],
                                                   ALU.subtract, ALU.mult)
                last.then_inc(z_ready, 1)

            def z_low(n):
                dve.wait_ge(zhi_ready, n.count(1, 1))
                nc.vector.tensor_tensor(zT_lo[:, n.parity], bankA[:], zT_hi[:, n.parity].bitcast(F32),
                                        ALU.subtract).then_inc(zlo_ready, 1)

            def wide(a):
                return a.unsqueeze(2).to_broadcast([P, T, E])

            def step(n, place, ins):
                ins.then_inc(top_step, 1)
                dve.wait_ge(top_step, n.count(TOP_STEPS, place))

            def logits(n):
                dve.wait_ge(lg_ps, n.count(1, 1))
                after(dve, top_step, n.count(TOP_STEPS, 0))
                parts = bankB[:, 0:T * 2 * E].rearrange("p (t r e) -> p t r e", t=T, r=2)
                step(n, 1, nc.vector.tensor_copy(lg[:, :, 0:E], parts[:, :, 1, :]))
                nc.vector.tensor_tensor(lg[:, :, 0:E], lg[:, :, 0:E], parts[:, :, 0, :], ALU.add).then_inc(lg_ready, 1)

            def top_two(n):
                dve.wait_ge(lg_ready, n.count(1, 1))
                nc.vector.memset(wait_cell[:], 0.0)
                for t in range(T):
                    last = nc.vector.max(top[:, t, :], lg[:, t, 0:E])
                step(n, 2, last)
                after(dve, th_ready, n.count(1, 0))
                nc.vector.tensor_tensor(gap[:], top[:, :, 0], top[:, :, 1], ALU.subtract).then_inc(gap_ready, 1)

            def choose(n):
                nc.vector.tensor_tensor(first_e[:], lg[:, :, 0:E], wide(top[:, :, 0]), ALU.is_equal)
                step(n, 3, nc.vector.memset(top[:, :, 2:8], LOWEST))
                nc.vector.memset(wait_cell[:], 0.0)
                for t in range(T):
                    last = nc.vector.match_replace(rest[:, t, :], top[:, t, :], lg[:, t, :], LOWEST)
                step(n, 4, last)
                step(n, 5, nc.vector.tensor_tensor(chosen[:], lg[:, :, 0:E], rest[:, :, 0:E], ALU.not_equal))

            def combine_weights(n):
                dve.wait_ge(th_ready, n.count(1, 1))
                step(n, 6, nc.vector.scalar_tensor_tensor(tilt[:], first_e[:], -0.5, wide(th[:]), ALU.add, ALU.mult))
                step(n, 7, nc.vector.scalar_tensor_tensor(cw[:], tilt[:], 0.5, chosen[:], ALU.add, ALU.mult))
                after(dve, cT_ps, n.count(1, 0))
                tiles = c_parts[:, :, 0:CR].rearrange("p t (q r e) -> p t q r e", q=2, e=E)
                twice = cw[:].unsqueeze(2).to_broadcast([P, T, 2, E])
                step(n, 8, nc.vector.tensor_copy(tiles[:, :, :, 0, :].bitcast(F32R), twice))
                nc.vector.tensor_tensor(tiles[:, :, :, 1, :], twice, tiles[:, :, :, 0, :],
                                        ALU.subtract).then_inc(top_step, 1)

            def weigh(i, e):
                dve.wait_ge(g_ready, i.count(E, e + 1))
                dve.wait_ge(cb_ps, i.count(E, e + 1))
                after(dve, lo_ready, i.count(E, e - 1))
                nc.vector.tensor_tensor(gc[:, e % 2, :], g_sb[:, e % 2, :], bankC[e % 2][:],
                                        ALU.mult).then_inc(gc_ready, 1)

            def low(i, e):
                dve.wait_ge(hi_ready, i.count(E, e + 1))
                nc.vector.tensor_tensor(gc_lo[:, e % 4, :], gc[:, e % 2, :], gc_hi[:, e % 4, :].bitcast(F32),
                                        ALU.subtract).then_inc(lo_ready, 1)

            def output(m):
                dve.wait_ge(o_ps, m.count(1, 1))
                dve.wait_ge(res_ready, m.count(1, 1))
                after(dve, o_stored, m.count(16, 0))
                nc.vector.tensor_tensor(o_sb[:], bankO[:].rearrange("p (t d) -> p t d", t=T), res[:, m.parity],
                                        ALU.add).then_inc(o_ready, 1)

            def setup(ins):
                setup.n += 1
                ins.then_inc(setup_dve, 1)
                dve.wait_ge(setup_dve, setup.n)

            def split(hi, lo, whole):
                setup(nc.vector.tensor_copy(hi, whole))
                setup(nc.vector.tensor_tensor(lo, whole, hi.bitcast(F32), ALU.subtract))

            setup.n = 0
            first = Step(None, 0)
            ln1_stat(first)
            dve.wait_ge(small_T_ps, 1)
            setup(nc.vector.tensor_copy(rwT[:], bankO[:, 0:E]))
            setup(nc.vector.tensor_copy(mb1T[:], bankO[:, E:2 * E]))
            setup(nc.vector.tensor_copy(b1_sb[:], bankO[:, 2 * E:2 * E + HC]))
            split(rwT_parts[:, 0:E], rwT_parts[:, E:2 * E], rwT[:])
            split(W1_hi[:], W1_lo[:], W1_sb[:])
            assert setup.n == SMALL_SETUPS
            a_low(first)
            dve.wait_ge(w_high, 1)
            setup(nc.vector.tensor_tensor(w1_lo[:], w1_sb[:], w1_hi[:].bitcast(F32), ALU.subtract))
            first_residual(first)
            ln2_stat(first)
            dve.wait_ge(b2_rows, 16 * 4)
            setup(nc.vector.tensor_copy(mb2[:], mb2_sb[:]))
            low_rows = slice(ROW_TILE, CR)
            setup(nc.vector.tensor_tensor(mb2[low_rows, :], mb2_sb[low_rows, :], mb2[low_rows, :].bitcast(F32),
                                          ALU.subtract))
            ln2_apply(first)
            ln1_stat(first.at(1))
            z_low(first)
            dve.wait_ge(pool_const, CONSTS)
            logits(first)
            top_two(first)
            choose(first)
            combine_weights(first)
            setup(nc.vector.tensor_copy(sel[:], sel_f[:]))
            assert setup.n == SETUPS
            dve.wait_ge(w_high, 2)
            nc.vector.tensor_tensor(w2_lo[:], w2_sb[:], w2_hi[:].bitcast(F32), ALU.subtract).then_inc(w2_split, 1)

            def iteration(i):
                b, n, f = i.at(-1), i.at(1), i.at(2)
                before, more, further = has(i, -1), has(i, 1), has(i, 2)
                if before:
                    low(b, 5)
                    weigh(b, 7)
                if more:
                    a_low(n)
                if before:
                    low(b, 6)
                weigh(i, 0)
                if before:
                    low(b, 7)
                weigh(i, 1)
                if further:
                    ln1_stat(f)
                low(i, 0)
                low(i, 1)
                if more:
                    first_residual(n)
                    ln2_stat(n)
                weigh(i, 2)
                weigh(i, 3)
                if more:
                    ln2_apply(n)
                low(i, 2)
                if before:
                    output(b)
                low(i, 3)
                if more:
                    z_low(n)
                weigh(i, 4)
                weigh(i, 5)
                if more:
                    logits(n)
                low(i, 4)
                if more:
                    top_two(n)
                    choose(n)
                weigh(i, 6)
                if more:
                    combine_weights(n)

            run(dve, iteration)
            last = Step(None, GROUPS - 1)
            low(last, 5)
            weigh(last, 7)
            low(last, 6)
            low(last, 7)
            output(last)

        @block.tensor
        def _(pe):
            def mm(out_ap, lhsT, rhs, start, stop):
                return nc.tensor.matmul(out_ap, lhsT, rhs, start=start, stop=stop)

            def three(out_ap, w_hi, w_lo, m_hi, m_lo, start, stop):
                mm(out_ap, w_lo, m_hi, start, False)
                mm(out_ap, w_hi, m_lo, False, False)
                return mm(out_ap, w_hi, m_hi, False, stop)

            def adj_transposes(n, g):
                pe.wait_ge(self_added, n.count(NC, NC))
                if g == 0:
                    after(pe, zlo_ready, n.count(1, 0))
                else:
                    after(pe, lg_ready, n.count(1, 0))
                bank = (bankA, bankB)[g]
                for c in range(NC):
                    for r in range(NC):
                        last = nc.tensor.transpose(bank[:, c * N + r * P:c * N + (r + 1) * P],
                                                   adj_sb[:, n.parity, g * NC + r, c * P:(c + 1) * P], ident[:])
                last.then_inc(adjT_ps, 1)

            def aggregate(n):
                pe.wait_ge(xn_ready, n.count(1, 1))
                pe.wait_ge(adjT_ready, n.count(GG, GG))
                for g in range(GG):
                    for c in range(NC):
                        last = mm(bankA[:, g * N:(g + 1) * N], xn[:, g * NC + c, :], adjT[:, g, c, :],
                                  c == 0, c == NC - 1)
                last.then_inc(agg_ps, 1)

            def ffn1(n, j):
                pe.wait_ge(ahi_ready, n.count(1, 1))
                pe.wait_ge(alo_ready, n.count(1, 1))
                cols = slice(j * P, (j + 1) * P)
                three((bankB, bankA)[j][:], W1_hi[:, cols], W1_lo[:, cols], aT_hi[:], aT_lo[:],
                      True, True).then_inc(f1_ps, 1)

            def ffn2(n):
                pe.wait_ge(hT_ready, n.count(HC, HC))
                for t in range(T):
                    for j in range(HC):
                        last = mm(bankB[:, t * D:(t + 1) * D], hT[:, j, t * P:(t + 1) * P], W2_sb[:, j, :],
                                  j == 0, j == HC - 1)
                last.then_inc(f2_ps, 1)

            def z_transposes(n):
                pe.wait_ge(z_ready, n.count(1, 1))
                for t in range(T):
                    last = nc.tensor.transpose(bankA[:, t * P:(t + 1) * P], z[:, t, :], ident[:])
                last.then_inc(zT_ps, 1)

            def router(n, t):
                if t == 0:
                    pe.wait_ge(zhi_ready, n.count(1, 1))
                    pe.wait_ge(zlo_ready, n.count(1, 1))
                    pe.wait_ge(x1_ready, n.count(1, 1))
                cols = slice(t * P, (t + 1) * P)
                at = t * 2 * E
                mm(bankB[:, at:at + 2 * E], zT_hi[:, n.parity, cols], rwT_parts[:], True, False)
                last = mm(bankB[:, at:at + E], zT_lo[:, n.parity, cols], rwT_parts[:, 0:E], False, True)
                if t == T - 1:
                    last.then_inc(lg_ps, 1)

            def weight_transposes(n):
                pe.wait_ge(top_step, n.count(TOP_STEPS, TOP_STEPS))
                after(pe, o_ready, n.count(1, -1))
                for t in range(T):
                    last = nc.tensor.transpose(bankO[:, t * P:(t + 1) * P], c_parts[:, t, :], ident[:])
                last.then_inc(cT_ps, 1)

            def spread(i, e):
                pe.wait_ge(cT_ready, i.count(1, 1))
                after(pe, gc_ready, i.count(E, e))
                for q in range(2):
                    rows = slice(q * ROW_TILE, q * ROW_TILE + 2 * E)
                    mm(bankC[q][:], sel[rows, e + q, :], cT[rows, :], True, True).then_inc(cb_ps, 1)

            def up(i, e):
                after(pe, g_ready, i.count(E, e - 1))
                if e == 0:
                    pe.wait_ge(zhi_ready, i.count(1, 1))
                    pe.wait_ge(zlo_ready, i.count(1, 1))
                three(bankH[e % 2][:], w1_hi[:, e, :], w1_lo[:, e, :], zT_hi[:, i.parity], zT_lo[:, i.parity],
                      True, True).then_inc(h_ps, 1)

            def down(i, e):
                pe.wait_ge(lo_ready, i.count(E, e + 1))
                if i.k is None and i.c == 0 and e == 0:
                    pe.wait_ge(w2_split, 1)
                if e == 0:
                    after(pe, yT_ready, i.count(1, 0))
                    mm(bankY[:], mb2[:], cT[:], True, False)
                three(bankY[:], w2_hi[:, e, :], w2_lo[:, e, :], gc_hi[:, e % 4, :], gc_lo[:, e % 4, :],
                      False, e == E - 1).then_inc(down_done, 1)

            def output_transposes(m):
                pe.wait_ge(yT_ready, m.count(1, 1))
                if has(m, 1):
                    pe.wait_ge(cT_ready, m.count(1, 2))
                else:
                    pe.wait_ge(o_ready, m.count(1, 0))
                for t in range(T):
                    last = nc.tensor.transpose(bankO[:, t * P:(t + 1) * P], yT[:, t * P:(t + 1) * P], ident[:])
                last.then_inc(o_ps, 1)

            pe.wait_ge(pool_const, 2)
            pe.wait_ge(gnn_weights, 16 * GNN_LOADS)
            nc.tensor.transpose(bankO[:, 0:E], rw_sb[:], ident[0:E, 0:E])
            nc.tensor.transpose(bankO[:, E:2 * E], mb1_sb[:], ident[0:E, 0:E])
            nc.tensor.transpose(bankO[:, 2 * E:2 * E + HC], b1_rows[:], ident[0:HC, 0:HC]).then_inc(small_T_ps, 1)
            first = Step(None, 0)
            for g in range(GG):
                adj_transposes(first, g)
            aggregate(first)
            pe.wait_ge(setup_dve, SMALL_SETUPS)
            for j in range(HC):
                ffn1(first, j)
            ffn2(first)
            z_transposes(first)
            pe.wait_ge(setup_dve, SMALL_SETUPS)
            for t in range(T):
                router(first, t)
            for g in range(GG):
                adj_transposes(first.at(1), g)
            pe.wait_ge(setup_dve, SETUPS)

            def iteration(i):
                b, n, f = i.at(-1), i.at(1), i.at(2)
                before, more, further = has(i, -1), has(i, 1), has(i, 2)
                if before:
                    down(b, 3)
                if more:
                    aggregate(n)
                weight_transposes(i)
                up(i, 0)
                up(i, 1)
                spread(i, 0)
                if more:
                    ffn1(n, 0)
                    ffn1(n, 1)
                if before:
                    down(b, 4)
                    down(b, 5)
                if more:
                    ffn2(n)
                up(i, 2)
                if before:
                    down(b, 6)
                up(i, 3)
                spread(i, 2)
                if before:
                    down(b, 7)
                up(i, 4)
                up(i, 5)
                down(i, 0)
                if before:
                    output_transposes(b)
                if more:
                    z_transposes(n)
                down(i, 1)
                spread(i, 4)
                up(i, 6)
                up(i, 7)
                if more:
                    router(n, 0)
                    router(n, 1)
                    router(n, 2)
                    router(n, 3)
                if further:
                    adj_transposes(f, 0)
                down(i, 2)
                if further:
                    adj_transposes(f, 1)
                spread(i, 6)

            run(pe, iteration)
            last = Step(None, GROUPS - 1)
            down(last, 3)
            down(last, 4)
            down(last, 5)
            down(last, 6)
            down(last, 7)
            output_transposes(last)


_INS = ['x', 'adj', 'L0_gnn_eps', 'L0_gnn_W1', 'L0_gnn_b1', 'L0_gnn_W2', 'L0_gnn_b2', 'L0_ffn_router_w',
        'L0_ffn_w1', 'L0_ffn_b1', 'L0_ffn_w2', 'L0_ffn_b2']


def kernel(**inputs):
    import numpy as _np
    import concourse.bacc as _bacc
    from concourse import mybir as _mybir
    from concourse.bass_utils import run_bass_kernel_spmd as _run

    nc = _bacc.Bacc("TRN2", target_bir_lowering=False, num_devices=1)
    arrays, args = {}, []
    for name in _INS:
        a = _np.ascontiguousarray(inputs[name])
        arrays[f"in_{name}"] = a
        args.append(nc.dram_tensor(f"in_{name}", a.shape, _mybir.dt.from_np(a.dtype), kind="ExternalInput").ap())
    shape = inputs['x'].shape
    args.append(nc.dram_tensor("out_0", shape, _mybir.dt.from_np(_np.dtype('float32')), kind="ExternalOutput").ap())
    gnn_moe_block(nc, *args)
    r = _run(nc, [arrays], core_ids=[0])
    return r.results[0]["out_0"]
```

```python
from contextlib import ExitStack

import concourse.bass as bass
from concourse import mybir

ALU = mybir.AluOpType
ACT = mybir.ActivationFunctionType
F32 = mybir.dt.float32
F32R = mybir.dt.float32r

P = 128
LN_EPS = 1e-5
LOWEST = -3.0e38


class Step:

    def __init__(self, k, c):
        self.k, self.c = k, c

    def at(self, off):
        return Step(self.k, self.c + off)

    @property
    def parity(self):
        return self.c % 2

    def index(self):
        return self.count(1, 0)

    def count(self, per_group, plus):
        fixed = per_group * self.c + plus
        return fixed if self.k is None else self.k * (2 * per_group) + fixed

    def loads(self):
        fixed = 16 * (self.c // 2 + 1)
        return fixed if self.k is None else self.k * 16 + fixed


def gnn_moe_block(nc, x, adj, eps, W1, b1, W2, b2, router_w, w1, mb1, w2, mb2_rows, out):
    G, N, D = x.shape
    H = W1.shape[1]
    E = router_w.shape[0]
    HC = H // P
    NC = N // P
    T = 4
    GG = T // NC
    GROUPS = G // GG
    TOK = T * P
    assert D == P and N == NC * P and H == HC * P and GG * NC == T and GROUPS % 2 == 0 and E == 8 and HC == 2
    DEPTH = 4
    ROW_TILE = 32
    CR = 2 * ROW_TILE

    x_rows = x.rearrange("g (c p) d -> p (g c) d", p=P)
    out_rows = out.rearrange("g (c p) d -> p (g c) d", p=P)
    adj_rows = adj.rearrange("g (c p) m -> p (g c) m", p=P)

    ctx = ExitStack()
    with ctx:
        def sb(name, shape, dt=F32):
            return ctx.enter_context(nc.sbuf_tensor(name, shape, dt))

        def psum(name, shape):
            return ctx.enter_context(nc.psum_tensor(name, shape, F32))

        def sem(name):
            return ctx.enter_context(nc.semaphore(name))

        ident = sb("ident", [P, P])
        diag = sb("diag", [P, P])
        eps1 = sb("eps1", [P, 1])
        half = sb("half", [P, T])
        minus = sb("minus", [P, T])
        ln_eps = sb("ln_eps", [P, T])
        W1_sb = sb("W1_sb", [P, H])
        W1_hi = sb("W1_hi", [P, H], F32R)
        W1_lo = sb("W1_lo", [P, H], F32R)
        b1_rows = sb("b1_rows", [HC, P])
        b1_sb = sb("b1_sb", [P, HC])
        W2_sb = sb("W2_sb", [P, HC, D])
        b2_bc = sb("b2_bc", [P, D])
        rw_sb = sb("rw_sb", [E, D])
        rwT = sb("rwT", [P, E])
        rwT_parts = sb("rwT_parts", [P, 2 * E], F32R)
        w1_sb = sb("w1_sb", [P, E, D])
        w1_hi = sb("w1_hi", [P, E, D], F32R)
        w1_lo = sb("w1_lo", [P, E, D], F32R)
        w2_sb = sb("w2_sb", [P, E, D])
        w2_hi = sb("w2_hi", [P, E, D], F32R)
        w2_lo = sb("w2_lo", [P, E, D], F32R)
        mb1_sb = sb("mb1_sb", [E, D])
        mb1T = sb("mb1T", [P, E])
        mb2_sb = sb("mb2_sb", [CR, D])
        mb2 = sb("mb2_parts", [CR, D], F32R)
        sel_f = sb("sel_f", [CR, E, P])
        sel = sb("sel", [CR, E, P], F32R)

        x_sb = sb("x_sb", [P, 2, T, D])
        adj_sb = sb("adj_sb", [P, 2, T, N])
        st1 = sb("st1", [P, T, 6])
        mv1 = sb("mv1", [P, T, 2])
        nm1 = sb("nm1", [P, T])
        ve1 = sb("ve1", [P, T])
        rs1 = sb("rs1", [P, T])
        nb1 = sb("nb1", [P, T])
        xn = sb("xn", [P, 2, T, D])
        xb = sb("xb", [P, T, D])
        adjT = sb("adjT", [P, GG, NC, N])
        aT_hi = sb("aT_hi", [P, TOK], F32R)
        aT_lo = sb("aT_lo", [P, TOK], F32R)
        hT = sb("hT", [P, HC, TOK])
        x1 = sb("x1", [P, T, D])
        st2 = sb("st2", [P, T, 6])
        mv2 = sb("mv2", [P, T, 2])
        ve2 = sb("ve2", [P, T])
        rs2 = sb("rs2", [P, T])
        z = sb("z", [P, T, D])
        res = sb("res", [P, 2, T, D])
        zT_hi = sb("zT_hi", [P, 2, TOK], F32R)
        zT_lo = sb("zT_lo", [P, 2, TOK], F32R)
        lg = sb("lg", [P, T, 2 * E])
        top = sb("top", [P, T, 8])
        gap = sb("gap", [P, T])
        th = sb("th", [P, T])
        rest = sb("rest", [P, T, 2 * E])
        chosen = sb("chosen", [P, T, E])
        first_e = sb("first_e", [P, T, E])
        tilt = sb("tilt", [P, T, E])
        cw = sb("cw", [P, T, E])
        c_parts = sb("c_parts", [P, T, P])
        cT = sb("cT", [CR, TOK], F32R)
        g_sb = sb("g_sb", [P, DEPTH, TOK])
        gc = sb("gc", [P, DEPTH, TOK])
        gc_hi = sb("gc_hi", [P, DEPTH, TOK], F32R)
        gc_lo = sb("gc_lo", [P, DEPTH, TOK], F32R)
        yT = sb("yT", [P, TOK])
        o_sb = sb("o_sb", [P, T, D])
        wait_cell = sb("wait_cell", [P, 2])

        bankA = psum("bankA", [P, TOK])
        bankB = psum("bankB", [P, TOK])
        bankO = psum("bankO", [P, TOK])
        bankH = [psum(f"bankH{j}", [P, TOK]) for j in range(2)]
        bankC = [psum(f"bankC{j}", [P, TOK]) for j in range(2)]
        bankY = psum("bankY", [P, TOK])

        class LoopBanks:
            adj, agg, hidden, result = (bankA, bankB), bankA, (bankB, bankA), bankB

        class StartBanks:
            adj, agg, hidden, result = bankH, bankC[0], (bankC[1], bankY), bankY

        def banks_of(n):
            return StartBanks if n.k is None and n.c == 1 else LoopBanks

        small_weights = sem("small_weights")
        W1_landed = sem("W1_landed")
        W2_landed = sem("W2_landed")
        b2_landed = sem("b2_landed")
        table_loaded = sem("table_loaded")
        w1_landed = sem("w1_landed")
        w2_landed = sem("w2_landed")
        b2_rows = sem("b2_rows")
        eps_landed = sem("eps_landed")
        w_high = sem("w_high")
        w2_split = sem("w2_split")
        pool_const = sem("pool_const")
        small_T_ps = sem("small_T_ps")
        setup_dve = sem("setup_dve")
        x_in = [sem(f"x_in{j}") for j in range(2)]
        adj_in = [sem(f"adj_in{j}") for j in range(2)]
        ln1_sub = sem("ln1_sub")
        ln1_stats = sem("ln1_stats")
        ln1_small = sem("ln1_small")
        xn_ready = sem("xn_ready")
        xb_ready = sem("xb_ready")
        self_added = sem("self_added")
        adjT_ps = sem("adjT_ps")
        adjT_ready = sem("adjT_ready")
        agg_ps = sem("agg_ps")
        ahi_ready = sem("ahi_ready")
        alo_ready = sem("alo_ready")
        f1_ps = sem("f1_ps")
        hT_ready = sem("hT_ready")
        f2_ps = sem("f2_ps")
        x1_ready = sem("x1_ready")
        ln2_sub = sem("ln2_sub")
        ln2_stats = sem("ln2_stats")
        ln2_small = sem("ln2_small")
        rs2_ready = sem("rs2_ready")
        z_ready = sem("z_ready")
        res_ready = sem("res_ready")
        zT_ps = sem("zT_ps")
        zhi_ready = sem("zhi_ready")
        zlo_ready = sem("zlo_ready")
        lg_ps = sem("lg_ps")
        lg_ready = sem("lg_ready")
        gap_ready = sem("gap_ready")
        th_ready = sem("th_ready")
        top_step = sem("top_step")
        cT_ps = sem("cT_ps")
        cT_ready = sem("cT_ready")
        cb_ps = sem("cb_ps")
        h_ps = sem("h_ps")
        g_ready = sem("g_ready")
        gc_ready = sem("gc_ready")
        hi_ready = sem("hi_ready")
        lo_ready = sem("lo_ready")
        down_done = sem("down_done")
        yT_ready = sem("yT_ready")
        o_ps = sem("o_ps")
        o_ready = sem("o_ready")
        o_stored = sem("o_stored")

        CLEARED, DIAG, CONSTS, SMALL_SETUPS, SETUPS, TOP_STEPS = 6, 8, 15, 7, 11, 9

        block = ctx.enter_context(nc.Block())

        def run(eng, first_iteration, iteration, last_iteration):
            first_iteration(Step(None, 0))
            iteration(Step(None, 1))
            with eng.Fori(0, (GROUPS - 4) // 2) as k:
                iteration(Step(k, 2))
                iteration(Step(k, 3))
            iteration(Step(None, GROUPS - 2))
            last_iteration(Step(None, GROUPS - 1))

        def has(s, off):
            return s.k is not None or 0 <= s.c + off < GROUPS

        def after(eng, what, count):
            if not isinstance(count, int) or count > 0:
                eng.wait_ge(what, count)

        def add_self(unit, eng, n):
            eng.wait_ge(adj_in[n.parity], n.loads())
            graphs = adj_sb[:, n.parity].rearrange("p (g c) m -> p g c m", g=GG)
            for c in range(NC):
                block_c = graphs[:, :, c, c * P:(c + 1) * P]
                unit.tensor_tensor(block_c, block_c, diag[:].unsqueeze(1).to_broadcast([P, GG, P]),
                                   ALU.add).then_inc(self_added, 1)

        @block.sync
        def _(sp):
            def rows(n, array):
                view = array[:, bass.ds(n.index() * T, T), :]
                if n.k is not None:
                    sp.lower_val(view.offset * 4)
                return view

            def load(n, x_view, adj_view):
                sp.dma_start(x_sb[:, n.parity], x_view).then_inc(x_in[n.parity], 16)
                sp.dma_start(adj_sb[:, n.parity], adj_view).then_inc(adj_in[n.parity], 16)

            def store(m, out_view):
                sp.wait_ge(o_ready, m.count(1, 1))
                sp.dma_start(out_view, o_sb[:]).then_inc(o_stored, 16)

            first = Step(None, 0)
            sp.dma_start(x_sb[:, 0], rows(first, x_rows)).then_inc(x_in[0], 16)
            sp.dma_start(eps1[:], eps.partition_broadcast(P)).then_inc(eps_landed, 16)
            sp.dma_start(adj_sb[:, 0], rows(first, adj_rows)).then_inc(adj_in[0], 16)
            second = first.at(1)
            load(second, rows(second, x_rows), rows(second, adj_rows))
            sp.dma_start(w1_sb[:], w1.rearrange("e d f -> d e f")).then_inc(w1_landed, 16)
            sp.dma_start(W2_sb[:], W2.rearrange("(j p) d -> p j d", p=P)).then_inc(W2_landed, 16)
            sp.dma_start(w2_sb[:], w2.rearrange("e f d -> f e d")).then_inc(w2_landed, 16)
            sp.wait_ge(pool_const, CLEARED)
            for row in (0, E, ROW_TILE, ROW_TILE + E):
                sp.dma_start(mb2_sb[row:row + E, :], mb2_rows).then_inc(b2_rows, 16)

            def iteration(i):
                if i.k is not None:
                    sp.lower_val(i.count(1, 1))
                    sp.lower_val(i.count(GG, GG))
                    sp.lower_val(i.count(1, 0))
                if has(i, 2):
                    x_view, adj_view = rows(i.at(2), x_rows), rows(i.at(2), adj_rows)
                if has(i, -1):
                    out_view = rows(i.at(-1), out_rows)
                if has(i, 2):
                    sp.wait_ge(xb_ready, i.count(1, 1))
                    sp.wait_ge(xn_ready, i.count(1, 1))
                    sp.wait_ge(adjT_ps, i.count(GG, GG))
                    load(i.at(2), x_view, adj_view)
                if has(i, -1):
                    store(i.at(-1), out_view)

            run(sp, iteration, iteration, iteration)
            last = Step(None, GROUPS - 1)
            store(last, rows(last, out_rows))
            sp.wait_ge(o_stored, 16 * GROUPS)

        @block.gpsimd
        def _(pool):
            def const(ins):
                const.n += 1
                ins.then_inc(pool_const, 1)
                pool.wait_ge(pool_const, const.n)

            def ln1_rstd(n):
                pool.wait_ge(ln1_stats, n.count(1, 1))
                after(pool, xn_ready, n.count(1, 0))
                nc.gpsimd.tensor_tensor(ve1[:], mv1[:, :, 1], ln_eps[:], ALU.add).then_inc(ln1_small, 1)
                nc.gpsimd.tensor_tensor(nm1[:], mv1[:, :, 0], minus[:], ALU.mult).then_inc(ln1_small, 1)
                pool.wait_ge(ln1_small, n.count(4, 2))
                nc.gpsimd.tensor_tensor(rs1[:], ve1[:], half[:], ALU.pow).then_inc(ln1_small, 1)
                pool.wait_ge(ln1_small, n.count(4, 3))
                nc.gpsimd.tensor_tensor(nb1[:], nm1[:], rs1[:], ALU.mult).then_inc(ln1_small, 1)

            def add_bias(n):
                after(pool, x1_ready, n.count(1, 0))
                nc.gpsimd.tensor_tensor(xb[:], x_sb[:, n.parity],
                                        b2_bc[:].unsqueeze(1).to_broadcast([P, T, D]), ALU.add).then_inc(xb_ready, 1)

            def ln2(n):
                pool.wait_ge(ln2_stats, n.count(1, 1))
                nc.gpsimd.tensor_tensor(ve2[:], mv2[:, :, 1], ln_eps[:], ALU.add).then_inc(ln2_small, 1)
                pool.wait_ge(ln2_small, n.count(1, 1))
                nc.gpsimd.tensor_tensor(rs2[:], ve2[:], half[:], ALU.pow).then_inc(rs2_ready, 1)

            def residual(n):
                pool.wait_ge(z_ready, n.count(1, 1))
                after(pool, o_ready, n.count(1, -1))
                nc.gpsimd.tensor_tensor(res[:, n.parity], x1[:], z[:], ALU.add).then_inc(res_ready, 1)

            const.n = 0
            const(nc.gpsimd.memset(ident[:], 0.0))
            const(nc.gpsimd.affine_select(out=ident[:], in_=ident[:], compare_op=ALU.not_equal, fill=1.0, base=0,
                                          pattern=[[-1, P]], channel_multiplier=1))
            const(nc.gpsimd.memset(half[:], -0.5))
            const(nc.gpsimd.memset(minus[:], -1.0))
            const(nc.gpsimd.memset(ln_eps[:], LN_EPS))
            const(nc.gpsimd.memset(mb2_sb[:], 0.0))
            assert const.n == CLEARED
            pool.wait_ge(eps_landed, 16)
            const(nc.gpsimd.tensor_scalar(eps1[:], eps1[:], 1.0, None, ALU.add))
            const(nc.gpsimd.tensor_scalar(diag[:], ident[:], eps1[:, 0:1], None, ALU.mult))
            assert const.n == DIAG
            first = Step(None, 0)
            ln1_rstd(first)
            const(nc.gpsimd.memset(sel_f[:], 0.0))
            for q in range(2):
                for part in range(2):
                    mine = sel_f[:].rearrange("r (h q) p -> r h q p", q=2)[:, :, q, :]
                    const(nc.gpsimd.affine_select(out=mine, in_=mine, compare_op=ALU.not_equal, fill=1.0,
                                                  base=-(ROW_TILE + 1) * q - E * part,
                                                  pattern=[[-2, E // 2], [0, P]], channel_multiplier=1))
            const(nc.gpsimd.memset(lg[:], LOWEST))
            ln1_rstd(first.at(1))
            pool.wait_ge(b2_landed, 16)
            add_bias(first)
            const(nc.gpsimd.memset(c_parts[:], 0.0))
            assert const.n == CONSTS
            pool.wait_ge(adjT_ps, GG)
            add_self(nc.gpsimd, pool, first.at(1))
            ln2(first)
            add_bias(first.at(1))
            residual(first)
            add_self(nc.gpsimd, pool, first.at(2))
            ln1_rstd(first.at(2))

            def first_iteration(i):
                ln2(i.at(1))
                residual(i.at(1))
                add_bias(i.at(2))

            def iteration(i):
                ln2(i.at(1))
                if has(i, 2):
                    add_self(nc.gpsimd, pool, i.at(2))
                    ln1_rstd(i.at(2))
                residual(i.at(1))
                if has(i, 2):
                    add_bias(i.at(2))

            def last_iteration(i):
                pass

            run(pool, first_iteration, iteration, last_iteration)

        @block.scalar
        def _(act):
            def adjT_copy(n, g):
                act.wait_ge(adjT_ps, n.count(GG, g + 1))
                after(act, agg_ps, n.count(1, 0))
                nc.scalar.activation(adjT[:, g].rearrange("p c n -> p (c n)"), banks_of(n).adj[g][:],
                                     ACT.Copy).then_inc(adjT_ready, 1)

            def aT_copy(n):
                act.wait_ge(agg_ps, n.count(1, 1))
                after(act, f1_ps, n.count(HC, 0))
                nc.scalar.activation(aT_hi[:], banks_of(n).agg[:], ACT.Copy).then_inc(ahi_ready, 1)

            def normalise(n):
                act.wait_ge(ln1_small, n.count(4, 4))
                after(act, agg_ps, n.count(1, -1))
                for t in range(T):
                    last = nc.scalar.activation(xn[:, n.parity, t, :], x_sb[:, n.parity, t, :], ACT.Identity,
                                                bias=nb1[:, t:t + 1], scale=rs1[:, t:t + 1])
                last.then_inc(xn_ready, 1)

            def hidden_relu(n, j):
                act.wait_ge(f1_ps, n.count(HC, j + 1))
                after(act, f2_ps, n.count(1, 0))
                nc.scalar.activation(hT[:, j, :], banks_of(n).hidden[j][:], ACT.Relu,
                                     bias=b1_sb[:, j:j + 1]).then_inc(hT_ready, 1)

            def z_high(n):
                act.wait_ge(zT_ps, n.count(1, 1))
                after(act, h_ps, n.count(E, -E))
                nc.scalar.activation(zT_hi[:, n.parity], bankA[:], ACT.Copy).then_inc(zhi_ready, 1)

            def gap_tanh(n):
                act.wait_ge(gap_ready, n.count(1, 1))
                nc.scalar.activation(th[:], gap[:], ACT.Tanh, scale=0.5).then_inc(th_ready, 1)

            def cT_copy(n):
                act.wait_ge(cT_ps, n.count(1, 1))
                after(act, cb_ps, n.count(E, 0))
                after(act, down_done, n.count(E, 1 - E))
                nc.scalar.activation(cT[:], bankO[0:CR, :], ACT.Copy).then_inc(cT_ready, 1)

            def gelu(i, e):
                act.wait_ge(h_ps, i.count(E, e + 1))
                after(act, gc_ready, i.count(E, e + 1 - DEPTH))
                nc.scalar.activation(g_sb[:, e % DEPTH, :], bankH[e % 2][:], ACT.Gelu,
                                     bias=mb1T[:, e:e + 1]).then_inc(g_ready, 1)

            def high(i, e):
                act.wait_ge(gc_ready, i.count(E, e + 1))
                after(act, down_done, i.count(E, e + 1 - DEPTH))
                nc.scalar.activation(gc_hi[:, e % DEPTH, :], gc[:, e % DEPTH, :], ACT.Copy).then_inc(hi_ready, 1)

            def yT_copy(i):
                act.wait_ge(down_done, i.count(E, E))
                after(act, o_ps, i.count(1, 0))
                nc.scalar.activation(yT[:], bankY[:], ACT.Copy).then_inc(yT_ready, 1)

            act.dma_start(rw_sb[:], router_w).then_inc(small_weights, 16)
            act.dma_start(mb1_sb[:], mb1).then_inc(small_weights, 16)
            act.dma_start(b1_rows[:], b1.rearrange("(j p) -> j p", p=P)).then_inc(small_weights, 16)
            act.dma_start(W1_sb[:], W1).then_inc(W1_landed, 16)
            act.dma_start(b2_bc[:], b2.partition_broadcast(P)).then_inc(b2_landed, 16)
            act.wait_ge(pool_const, CLEARED)
            nc.scalar.activation(th[:], half[:], ACT.Gelu).then_inc(table_loaded, 1)

            first = Step(None, 0)
            for g in range(GG):
                adjT_copy(first, g)
            act.wait_ge(w1_landed, 16)
            nc.scalar.activation(w1_hi[:], w1_sb[:], ACT.Copy).then_inc(w_high, 1)
            aT_copy(first)
            act.wait_ge(setup_dve, SMALL_SETUPS)
            for j in range(HC):
                hidden_relu(first, j)
            second = first.at(1)
            for g in range(GG):
                adjT_copy(second, g)
            act.wait_ge(w2_landed, 16)
            nc.scalar.activation(w2_hi[:], w2_sb[:], ACT.Copy).then_inc(w_high, 1)
            aT_copy(second)
            for j in range(HC):
                hidden_relu(second, j)
            z_high(first)
            act.wait_ge(table_loaded, 1)
            gap_tanh(first)

            def first_iteration(i):
                n, f = i.at(1), i.at(2)
                gelu(i, 0)
                gelu(i, 1)
                cT_copy(i)
                high(i, 0)
                high(i, 1)
                gelu(i, 2)
                gelu(i, 3)
                gelu(i, 4)
                z_high(n)
                high(i, 2)
                high(i, 3)
                gelu(i, 5)
                high(i, 4)
                normalise(f)
                gelu(i, 6)
                gap_tanh(n)
                adjT_copy(f, 0)
                gelu(i, 7)
                adjT_copy(f, 1)
                high(i, 5)
                high(i, 6)

            def iteration(i):
                b, n, f = i.at(-1), i.at(1), i.at(2)
                further = has(i, 2)
                gelu(i, 0)
                aT_copy(n)
                cT_copy(i)
                high(b, 7)
                gelu(i, 1)
                hidden_relu(n, 0)
                hidden_relu(n, 1)
                high(i, 0)
                high(i, 1)
                gelu(i, 2)
                gelu(i, 3)
                yT_copy(b)
                high(i, 2)
                gelu(i, 4)
                gelu(i, 5)
                high(i, 3)
                z_high(n)
                gelu(i, 6)
                high(i, 4)
                if further:
                    normalise(f)
                    adjT_copy(f, 0)
                gap_tanh(n)
                if further:
                    adjT_copy(f, 1)
                gelu(i, 7)
                high(i, 5)
                high(i, 6)

            def last_iteration(i):
                b = i.at(-1)
                gelu(i, 0)
                gelu(i, 1)
                cT_copy(i)
                high(b, 7)
                high(i, 0)
                high(i, 1)
                gelu(i, 2)
                gelu(i, 3)
                yT_copy(b)
                high(i, 2)
                gelu(i, 4)
                high(i, 3)
                gelu(i, 5)
                high(i, 4)
                gelu(i, 6)
                high(i, 5)
                gelu(i, 7)
                high(i, 6)
                high(i, 7)
                yT_copy(i)

            run(act, first_iteration, iteration, last_iteration)

        @block.vector
        def _(dve):
            def ln1_stat(n):
                dve.wait_ge(x_in[n.parity], n.loads())
                for t in range(T):
                    last = nc.vector.bn_stats(st1[:, t, :], x_sb[:, n.parity, t, :])
                last.then_inc(ln1_sub, 1)
                after(dve, xn_ready, n.count(1, 0))
                dve.wait_ge(ln1_sub, n.count(1, 1))
                nc.vector.memset(wait_cell[:], 0.0)
                for t in range(T):
                    last = nc.vector.bn_aggr(mv1[:, t, :], st1[:, t, :])
                last.then_inc(ln1_stats, 1)

            def normalise(n):
                dve.wait_ge(ln1_small, n.count(4, 4))
                for t in range(T):
                    last = nc.vector.tensor_scalar(xn[:, n.parity, t, :], x_sb[:, n.parity, t, :], nm1[:, t:t + 1],
                                                   rs1[:, t:t + 1], ALU.add, ALU.mult)
                last.then_inc(xn_ready, 1)

            def a_low(n):
                dve.wait_ge(ahi_ready, n.count(1, 1))
                nc.vector.tensor_tensor(aT_lo[:], banks_of(n).agg[:], aT_hi[:].bitcast(F32),
                                        ALU.subtract).then_inc(alo_ready, 1)

            def first_residual(n):
                dve.wait_ge(f2_ps, n.count(1, 1))
                dve.wait_ge(xb_ready, n.count(1, 1))
                after(dve, res_ready, n.count(1, 0))
                nc.vector.tensor_tensor(x1[:], banks_of(n).result[:].rearrange("p (t d) -> p t d", t=T), xb[:],
                                        ALU.add).then_inc(x1_ready, 1)

            def ln2_stat(n):
                dve.wait_ge(x1_ready, n.count(1, 1))
                for t in range(T):
                    last = nc.vector.bn_stats(st2[:, t, :], x1[:, t, :])
                last.then_inc(ln2_sub, 1)
                dve.wait_ge(ln2_sub, n.count(1, 1))
                nc.vector.memset(wait_cell[:], 0.0)
                for t in range(T):
                    last = nc.vector.bn_aggr(mv2[:, t, :], st2[:, t, :])
                last.then_inc(ln2_stats, 1)

            def ln2_apply(n):
                dve.wait_ge(rs2_ready, n.count(1, 1))
                dve.wait_ge(ln2_stats, n.count(1, 1))
                after(dve, zT_ps, n.count(1, 0))
                for t in range(T):
                    last = nc.vector.tensor_scalar(z[:, t, :], x1[:, t, :], mv2[:, t, 0:1], rs2[:, t:t + 1],
                                                   ALU.subtract, ALU.mult)
                last.then_inc(z_ready, 1)

            def z_low(n):
                dve.wait_ge(zhi_ready, n.count(1, 1))
                nc.vector.tensor_tensor(zT_lo[:, n.parity], bankA[:], zT_hi[:, n.parity].bitcast(F32),
                                        ALU.subtract).then_inc(zlo_ready, 1)

            def wide(a):
                return a.unsqueeze(2).to_broadcast([P, T, E])

            def step(n, place, ins):
                ins.then_inc(top_step, 1)
                dve.wait_ge(top_step, n.count(TOP_STEPS, place))

            def logits(n):
                dve.wait_ge(lg_ps, n.count(1, 1))
                after(dve, top_step, n.count(TOP_STEPS, 0))
                parts = bankB[:, 0:T * 2 * E].rearrange("p (t r e) -> p t r e", t=T, r=2)
                step(n, 1, nc.vector.tensor_copy(lg[:, :, 0:E], parts[:, :, 1, :]))
                nc.vector.tensor_tensor(lg[:, :, 0:E], lg[:, :, 0:E], parts[:, :, 0, :], ALU.add).then_inc(lg_ready, 1)

            def top_two(n):
                dve.wait_ge(lg_ready, n.count(1, 1))
                nc.vector.memset(wait_cell[:], 0.0)
                for t in range(T):
                    last = nc.vector.max(top[:, t, :], lg[:, t, 0:E])
                step(n, 2, last)
                after(dve, th_ready, n.count(1, 0))
                nc.vector.tensor_tensor(gap[:], top[:, :, 0], top[:, :, 1], ALU.subtract).then_inc(gap_ready, 1)

            def choose(n):
                nc.vector.tensor_tensor(first_e[:], lg[:, :, 0:E], wide(top[:, :, 0]), ALU.is_equal)
                step(n, 3, nc.vector.memset(top[:, :, 2:8], LOWEST))
                nc.vector.memset(wait_cell[:], 0.0)
                for t in range(T):
                    last = nc.vector.match_replace(rest[:, t, :], top[:, t, :], lg[:, t, :], LOWEST)
                step(n, 4, last)
                step(n, 5, nc.vector.tensor_tensor(chosen[:], lg[:, :, 0:E], rest[:, :, 0:E], ALU.not_equal))

            def combine_weights(n):
                dve.wait_ge(th_ready, n.count(1, 1))
                step(n, 6, nc.vector.scalar_tensor_tensor(tilt[:], first_e[:], -0.5, wide(th[:]), ALU.add, ALU.mult))
                step(n, 7, nc.vector.scalar_tensor_tensor(cw[:], tilt[:], 0.5, chosen[:], ALU.add, ALU.mult))
                after(dve, cT_ps, n.count(1, 0))
                tiles = c_parts[:, :, 0:CR].rearrange("p t (q r e) -> p t q r e", q=2, e=E)
                twice = cw[:].unsqueeze(2).to_broadcast([P, T, 2, E])
                step(n, 8, nc.vector.tensor_copy(tiles[:, :, :, 0, :].bitcast(F32R), twice))
                nc.vector.tensor_tensor(tiles[:, :, :, 1, :], twice, tiles[:, :, :, 0, :],
                                        ALU.subtract).then_inc(top_step, 1)

            def weigh(i, e):
                dve.wait_ge(g_ready, i.count(E, e + 1))
                dve.wait_ge(cb_ps, i.count(E, e + 1))
                after(dve, lo_ready, i.count(E, e + 1 - DEPTH))
                nc.vector.tensor_tensor(gc[:, e % DEPTH, :], g_sb[:, e % DEPTH, :], bankC[e % 2][:],
                                        ALU.mult).then_inc(gc_ready, 1)

            def low(i, e):
                dve.wait_ge(hi_ready, i.count(E, e + 1))
                nc.vector.tensor_tensor(gc_lo[:, e % DEPTH, :], gc[:, e % DEPTH, :], gc_hi[:, e % DEPTH, :].bitcast(F32),
                                        ALU.subtract).then_inc(lo_ready, 1)

            def output(m):
                dve.wait_ge(o_ps, m.count(1, 1))
                dve.wait_ge(res_ready, m.count(1, 1))
                after(dve, o_stored, m.count(16, 0))
                nc.vector.tensor_tensor(o_sb[:], bankO[:].rearrange("p (t d) -> p t d", t=T), res[:, m.parity],
                                        ALU.add).then_inc(o_ready, 1)

            def setup(ins):
                setup.n += 1
                ins.then_inc(setup_dve, 1)
                dve.wait_ge(setup_dve, setup.n)

            def split(hi, lo, whole):
                setup(nc.vector.tensor_copy(hi, whole))
                setup(nc.vector.tensor_tensor(lo, whole, hi.bitcast(F32), ALU.subtract))

            setup.n = 0
            first = Step(None, 0)
            ln1_stat(first)
            dve.wait_ge(pool_const, DIAG)
            add_self(nc.vector, dve, first)
            normalise(first)
            dve.wait_ge(small_T_ps, 1)
            setup(nc.vector.tensor_copy(rwT[:], bankO[:, 0:E]))
            setup(nc.vector.tensor_copy(mb1T[:], bankO[:, E:2 * E]))
            setup(nc.vector.tensor_copy(b1_sb[:], bankO[:, 2 * E:2 * E + HC]))
            split(rwT_parts[:, 0:E], rwT_parts[:, E:2 * E], rwT[:])
            dve.wait_ge(W1_landed, 16)
            split(W1_hi[:], W1_lo[:], W1_sb[:])
            assert setup.n == SMALL_SETUPS
            ln1_stat(first.at(1))
            normalise(first.at(1))
            a_low(first)
            dve.wait_ge(w_high, 1)
            setup(nc.vector.tensor_tensor(w1_lo[:], w1_sb[:], w1_hi[:].bitcast(F32), ALU.subtract))
            dve.wait_ge(b2_rows, 16 * 4)
            setup(nc.vector.tensor_copy(mb2[:], mb2_sb[:]))
            low_rows = slice(ROW_TILE, CR)
            setup(nc.vector.tensor_tensor(mb2[low_rows, :], mb2_sb[low_rows, :], mb2[low_rows, :].bitcast(F32),
                                          ALU.subtract))
            dve.wait_ge(pool_const, CONSTS)
            setup(nc.vector.tensor_copy(sel[:], sel_f[:]))
            assert setup.n == SETUPS
            ln1_stat(first.at(2))
            first_residual(first)
            ln2_stat(first)
            a_low(first.at(1))
            ln2_apply(first)
            dve.wait_ge(w_high, 2)
            nc.vector.tensor_tensor(w2_lo[:], w2_sb[:], w2_hi[:].bitcast(F32), ALU.subtract).then_inc(w2_split, 1)
            z_low(first)
            logits(first)
            top_two(first)
            choose(first)
            combine_weights(first)

            def first_iteration(i):
                n = i.at(1)
                first_residual(n)
                ln2_stat(n)
                weigh(i, 0)
                weigh(i, 1)
                low(i, 0)
                ln2_apply(n)
                weigh(i, 2)
                low(i, 1)
                weigh(i, 3)
                z_low(n)
                low(i, 2)
                weigh(i, 4)
                low(i, 3)
                weigh(i, 5)
                logits(n)
                low(i, 4)
                top_two(n)
                choose(n)
                weigh(i, 6)
                combine_weights(n)
                weigh(i, 7)

            def iteration(i):
                b, n, f = i.at(-1), i.at(1), i.at(2)
                further = has(i, 2)
                a_low(n)
                low(b, 5)
                weigh(i, 0)
                low(b, 6)
                low(b, 7)
                weigh(i, 1)
                low(i, 0)
                low(i, 1)
                first_residual(n)
                ln2_stat(n)
                weigh(i, 2)
                weigh(i, 3)
                ln2_apply(n)
                if further:
                    ln1_stat(f)
                output(b)
                z_low(n)
                weigh(i, 4)
                low(i, 2)
                weigh(i, 5)
                logits(n)
                low(i, 3)
                top_two(n)
                choose(n)
                weigh(i, 6)
                combine_weights(n)
                weigh(i, 7)
                low(i, 4)

            def last_iteration(i):
                b = i.at(-1)
                low(b, 5)
                low(b, 6)
                weigh(i, 0)
                low(b, 7)
                weigh(i, 1)
                low(i, 0)
                low(i, 1)
                weigh(i, 2)
                weigh(i, 3)
                low(i, 2)
                weigh(i, 4)
                low(i, 3)
                weigh(i, 5)
                low(i, 4)
                output(b)
                weigh(i, 6)
                low(i, 5)
                weigh(i, 7)
                low(i, 6)
                low(i, 7)
                output(i)

            run(dve, first_iteration, iteration, last_iteration)

        @block.tensor
        def _(pe):
            def mm(out_ap, lhsT, rhs, start, stop):
                return nc.tensor.matmul(out_ap, lhsT, rhs, start=start, stop=stop)

            def three(out_ap, w_hi, w_lo, m_hi, m_lo, start, stop):
                mm(out_ap, w_lo, m_hi, start, False)
                mm(out_ap, w_hi, m_lo, False, False)
                return mm(out_ap, w_hi, m_hi, False, stop)

            def adj_transposes(n, g):
                pe.wait_ge(self_added, n.count(NC, NC))
                bank = banks_of(n).adj[g]
                if bank is bankA:
                    after(pe, zlo_ready, n.count(1, 0))
                if bank is bankB:
                    after(pe, lg_ready, n.count(1, 0))
                for c in range(NC):
                    for r in range(NC):
                        last = nc.tensor.transpose(bank[:, c * N + r * P:c * N + (r + 1) * P],
                                                   adj_sb[:, n.parity, g * NC + r, c * P:(c + 1) * P], ident[:])
                last.then_inc(adjT_ps, 1)

            def aggregate(n):
                pe.wait_ge(xn_ready, n.count(1, 1))
                pe.wait_ge(adjT_ready, n.count(GG, GG))
                for g in range(GG):
                    for c in range(NC):
                        last = mm(banks_of(n).agg[:, g * N:(g + 1) * N], xn[:, n.parity, g * NC + c, :],
                                  adjT[:, g, c, :], c == 0, c == NC - 1)
                last.then_inc(agg_ps, 1)

            def ffn1(n, j):
                pe.wait_ge(ahi_ready, n.count(1, 1))
                pe.wait_ge(alo_ready, n.count(1, 1))
                cols = slice(j * P, (j + 1) * P)
                three(banks_of(n).hidden[j][:], W1_hi[:, cols], W1_lo[:, cols], aT_hi[:], aT_lo[:],
                      True, True).then_inc(f1_ps, 1)

            def ffn2(n):
                pe.wait_ge(hT_ready, n.count(HC, HC))
                for t in range(T):
                    for j in range(HC):
                        last = mm(banks_of(n).result[:, t * D:(t + 1) * D], hT[:, j, t * P:(t + 1) * P], W2_sb[:, j, :],
                                  j == 0, j == HC - 1)
                last.then_inc(f2_ps, 1)

            def z_transposes(n):
                pe.wait_ge(z_ready, n.count(1, 1))
                for t in range(T):
                    last = nc.tensor.transpose(bankA[:, t * P:(t + 1) * P], z[:, t, :], ident[:])
                last.then_inc(zT_ps, 1)

            def router(n, t):
                if t == 0:
                    pe.wait_ge(zhi_ready, n.count(1, 1))
                    pe.wait_ge(zlo_ready, n.count(1, 1))
                    pe.wait_ge(x1_ready, n.count(1, 1))
                cols = slice(t * P, (t + 1) * P)
                at = t * 2 * E
                mm(bankB[:, at:at + 2 * E], zT_hi[:, n.parity, cols], rwT_parts[:], True, False)
                last = mm(bankB[:, at:at + E], zT_lo[:, n.parity, cols], rwT_parts[:, 0:E], False, True)
                if t == T - 1:
                    last.then_inc(lg_ps, 1)

            def weight_transposes(n):
                pe.wait_ge(top_step, n.count(TOP_STEPS, TOP_STEPS))
                after(pe, o_ready, n.count(1, -1))
                for t in range(T):
                    last = nc.tensor.transpose(bankO[:, t * P:(t + 1) * P], c_parts[:, t, :], ident[:])
                last.then_inc(cT_ps, 1)

            def spread(i, e):
                pe.wait_ge(cT_ready, i.count(1, 1))
                after(pe, gc_ready, i.count(E, e))
                for q in range(2):
                    rows = slice(q * ROW_TILE, q * ROW_TILE + 2 * E)
                    mm(bankC[q][:], sel[rows, e + q, :], cT[rows, :], True, True).then_inc(cb_ps, 1)

            def up(i, e):
                after(pe, g_ready, i.count(E, e - 1))
                if e == 0:
                    pe.wait_ge(zhi_ready, i.count(1, 1))
                    pe.wait_ge(zlo_ready, i.count(1, 1))
                three(bankH[e % 2][:], w1_hi[:, e, :], w1_lo[:, e, :], zT_hi[:, i.parity], zT_lo[:, i.parity],
                      True, True).then_inc(h_ps, 1)

            def down(i, e):
                pe.wait_ge(lo_ready, i.count(E, e + 1))
                if i.k is None and i.c == 0 and e == 0:
                    pe.wait_ge(w2_split, 1)
                if e == 0:
                    after(pe, yT_ready, i.count(1, 0))
                    mm(bankY[:], mb2[:], cT[:], True, False)
                three(bankY[:], w2_hi[:, e, :], w2_lo[:, e, :], gc_hi[:, e % DEPTH, :], gc_lo[:, e % DEPTH, :],
                      False, e == E - 1).then_inc(down_done, 1)

            def output_transposes(m):
                pe.wait_ge(yT_ready, m.count(1, 1))
                if has(m, 1):
                    pe.wait_ge(cT_ready, m.count(1, 2))
                else:
                    pe.wait_ge(o_ready, m.count(1, 0))
                for t in range(T):
                    last = nc.tensor.transpose(bankO[:, t * P:(t + 1) * P], yT[:, t * P:(t + 1) * P], ident[:])
                last.then_inc(o_ps, 1)

            pe.wait_ge(pool_const, 2)
            pe.wait_ge(small_weights, 16 * 3)
            nc.tensor.transpose(bankO[:, 0:E], rw_sb[:], ident[0:E, 0:E])
            nc.tensor.transpose(bankO[:, E:2 * E], mb1_sb[:], ident[0:E, 0:E])
            nc.tensor.transpose(bankO[:, 2 * E:2 * E + HC], b1_rows[:], ident[0:HC, 0:HC]).then_inc(small_T_ps, 1)
            first = Step(None, 0)
            for g in range(GG):
                adj_transposes(first, g)
            aggregate(first)
            pe.wait_ge(setup_dve, SMALL_SETUPS)
            for j in range(HC):
                ffn1(first, j)
            second = first.at(1)
            for g in range(GG):
                adj_transposes(second, g)
            pe.wait_ge(W2_landed, 16)
            ffn2(first)
            aggregate(second)
            for j in range(HC):
                ffn1(second, j)
            z_transposes(first)
            ffn2(second)
            for t in range(T):
                router(first, t)
            pe.wait_ge(setup_dve, SETUPS)

            def first_iteration(i):
                n, f = i.at(1), i.at(2)
                up(i, 0)
                up(i, 1)
                weight_transposes(i)
                spread(i, 0)
                up(i, 2)
                up(i, 3)
                spread(i, 2)
                pe.wait_ge(x1_ready, n.count(1, 1))
                down(i, 0)
                up(i, 4)
                z_transposes(n)
                down(i, 1)
                up(i, 5)
                spread(i, 4)
                up(i, 6)
                router(n, 0)
                router(n, 1)
                router(n, 2)
                router(n, 3)
                up(i, 7)
                adj_transposes(f, 0)
                down(i, 2)
                spread(i, 6)
                adj_transposes(f, 1)

            def iteration(i):
                b, n, f = i.at(-1), i.at(1), i.at(2)
                further = has(i, 2)
                down(b, 3)
                up(i, 0)
                aggregate(n)
                weight_transposes(i)
                up(i, 1)
                up(i, 2)
                spread(i, 0)
                ffn1(n, 0)
                ffn1(n, 1)
                down(b, 4)
                down(b, 5)
                ffn2(n)
                spread(i, 2)
                down(b, 6)
                up(i, 3)
                down(b, 7)
                up(i, 4)
                up(i, 5)
                down(i, 0)
                output_transposes(b)
                spread(i, 4)
                z_transposes(n)
                up(i, 6)
                down(i, 1)
                up(i, 7)
                router(n, 0)
                router(n, 1)
                router(n, 2)
                router(n, 3)
                if further:
                    adj_transposes(f, 0)
                down(i, 2)
                spread(i, 6)
                if further:
                    adj_transposes(f, 1)

            def last_iteration(i):
                b = i.at(-1)
                down(b, 3)
                up(i, 0)
                up(i, 1)
                weight_transposes(i)
                down(b, 4)
                spread(i, 0)
                down(b, 5)
                up(i, 2)
                down(b, 6)
                up(i, 3)
                spread(i, 2)
                down(b, 7)
                up(i, 4)
                spread(i, 4)
                down(i, 0)
                up(i, 5)
                down(i, 1)
                output_transposes(b)
                up(i, 6)
                spread(i, 6)
                up(i, 7)
                down(i, 2)
                down(i, 3)
                down(i, 4)
                down(i, 5)
                down(i, 6)
                down(i, 7)
                output_transposes(i)

            run(pe, first_iteration, iteration, last_iteration)


_INS = ['x', 'adj', 'L0_gnn_eps', 'L0_gnn_W1', 'L0_gnn_b1', 'L0_gnn_W2', 'L0_gnn_b2', 'L0_ffn_router_w',
        'L0_ffn_w1', 'L0_ffn_b1', 'L0_ffn_w2', 'L0_ffn_b2']


def kernel(**inputs):
    import numpy as _np
    import concourse.bacc as _bacc
    from concourse import mybir as _mybir
    from concourse.bass_utils import run_bass_kernel_spmd as _run

    nc = _bacc.Bacc("TRN2", target_bir_lowering=False, num_devices=1)
    arrays, args = {}, []
    for name in _INS:
        a = _np.ascontiguousarray(inputs[name])
        arrays[f"in_{name}"] = a
        args.append(nc.dram_tensor(f"in_{name}", a.shape, _mybir.dt.from_np(a.dtype), kind="ExternalInput").ap())
    shape = inputs['x'].shape
    args.append(nc.dram_tensor("out_0", shape, _mybir.dt.from_np(_np.dtype('float32')), kind="ExternalOutput").ap())
    gnn_moe_block(nc, *args)
    r = _run(nc, [arrays], core_ids=[0])
    return r.results[0]["out_0"]
```
